# Optimizing a Trainium2 kernel written in Bass

```python
import numpy as np
import jax
import jax.numpy as jnp

def _softmax(x, axis=-1):
    return jax.nn.softmax(x, axis=axis)

def _gelu(x):
    return jax.nn.gelu(x, approximate=True)

def _silu(x):
    return jax.nn.silu(x)

def _sigmoid(x):
    return jax.nn.sigmoid(x)

def _layernorm(x, axis=-1, eps=1e-05):
    m = jnp.mean(x, axis=axis, keepdims=True)
    v = jnp.var(x, axis=axis, keepdims=True)
    return (x - m) / jnp.sqrt(v + eps)

def _scatter_add(tgt, idx, src, axis=0):
    return tgt.at[idx].add(src)

def _segment_sum(src, seg, n):
    return jax.ops.segment_sum(src, seg, n)
kernel_name = 'mk_metaformer_d1_conv_nhwc128_r2_3d5edc'

def setup_inputs(seed: int=0):
    np.random.seed(seed)
    _w = jnp.asarray

    def _rec_inputs():
        import jax
        import jax.numpy as jnp
        _gk = jax.random.key(seed)
        x = -0.0003972 + 0.9999 * jax.random.normal(jax.random.fold_in(_gk, 1), (1, 160, 160, 64), jnp.float32)
        return x
    x = _rec_inputs()

    def _L0_conv_setup():
        import jax, jax.numpy as jnp
        import numpy as np
        B, N, D, H, DH = (1, 160, 64, 4, 32)
        INNER = H * DH
        key = jax.random.key(seed)
        ks = jax.random.split(key, 7)
        sd = D ** (-0.5)
        return {'pairwise_repr': jax.random.normal(ks[0], (B, N, N, D), dtype=jnp.float32), 'mask': jnp.ones((B, N), dtype=bool), 'Wq': jax.random.normal(ks[1], (D, INNER), dtype=jnp.float32) * sd, 'Wk': jax.random.normal(ks[2], (D, INNER), dtype=jnp.float32) * sd, 'Wv': jax.random.normal(ks[3], (D, INNER), dtype=jnp.float32) * sd, 'Wg': jax.random.normal(ks[4], (D, INNER), dtype=jnp.float32) * sd, 'Wo': jax.random.normal(ks[5], (INNER, D), dtype=jnp.float32) * INNER ** (-0.5), 'Wb': jax.random.normal(ks[6], (D, H), dtype=jnp.float32) * sd}
    _L0_conv_all = _L0_conv_setup()
    _L0_conv_in = {k: v for k, v in _L0_conv_all.items() if k in ('mask', 'Wq', 'Wk', 'Wv', 'Wg', 'Wo', 'Wb')}
    del _L0_conv_all

    def _L0_ffn_setup():
        import jax, jax.numpy as jnp
        import numpy as np
        B, N, D, C, E, K = (8, 4096, 64, 64, 8, 2)
        key = jax.random.key(seed)
        k0, k1, k2 = jax.random.split(key, 3)
        x = jax.random.normal(k0, (B, N, D), dtype=jnp.float32)
        router_w = jax.random.normal(k1, (D, E), dtype=jnp.float32) * 0.05
        router_b = jnp.zeros((E,), dtype=jnp.float32)
        expert_w = jax.random.normal(k2, (E, D, C), dtype=jnp.float32) * (1.0 / np.sqrt(D))
        expert_b = jnp.zeros((E, C), dtype=jnp.float32)
        return {'x': x, 'router_w': router_w, 'router_b': router_b, 'expert_w': expert_w, 'expert_b': expert_b}
    _L0_ffn_all = _L0_ffn_setup()
    _L0_ffn_in = {k: v for k, v in _L0_ffn_all.items() if k in ('router_w', 'router_b', 'expert_w', 'expert_b')}
    del _L0_ffn_all
    return {'x': x, 'L0_conv_mask': _L0_conv_in['mask'], 'L0_conv_Wq': _L0_conv_in['Wq'], 'L0_conv_Wk': _L0_conv_in['Wk'], 'L0_conv_Wv': _L0_conv_in['Wv'], 'L0_conv_Wg': _L0_conv_in['Wg'], 'L0_conv_Wo': _L0_conv_in['Wo'], 'L0_conv_Wb': _L0_conv_in['Wb'], 'L0_ffn_router_w': _L0_ffn_in['router_w'], 'L0_ffn_router_b': _L0_ffn_in['router_b'], 'L0_ffn_expert_w': _L0_ffn_in['expert_w'], 'L0_ffn_expert_b': _L0_ffn_in['expert_b']}

def reference(x, L0_conv_mask, L0_conv_Wq, L0_conv_Wk, L0_conv_Wv, L0_conv_Wg, L0_conv_Wo, L0_conv_Wb, L0_ffn_router_w, L0_ffn_router_b, L0_ffn_expert_w, L0_ffn_expert_b):
    import jax
    import jax.numpy as jnp

    def _L0_conv_ref(pairwise_repr, mask, Wq, Wk, Wv, Wg, Wo, Wb):
        import jax, jax.numpy as jnp
        import numpy as np
        B, N, D, H, DH = (1, 160, 64, 4, 32)
        INNER = H * DH
        b, n, _, d = pairwise_repr.shape
        h = Wb.shape[1]
        inner = Wq.shape[1]
        dh = inner // h
        scale = dh ** (-0.5)
        bias = jnp.einsum('bijd,dh->bhij', pairwise_repr, Wb)
        q = jnp.einsum('brjd,de->brje', pairwise_repr, Wq).reshape(b, n, n, h, dh)
        k = jnp.einsum('brjd,de->brje', pairwise_repr, Wk).reshape(b, n, n, h, dh)
        v = jnp.einsum('brjd,de->brje', pairwise_repr, Wv).reshape(b, n, n, h, dh)
        sim = jnp.einsum('brihe,brjhe->brhij', q, k) * scale
        sim = sim + bias[:, None]
        sim = jnp.where(mask[:, None, None, None, :], sim, jnp.float32(-1000000000.0))
        attn = jax.nn.softmax(sim, axis=-1)
        o = jnp.einsum('brhij,brjhe->brihe', attn, v).reshape(b, n, n, inner)
        gates = jax.nn.sigmoid(jnp.einsum('brid,de->brie', pairwise_repr, Wg))
        out = jnp.einsum('brie,ed->brid', o * gates, Wo)
        return out

    def _L0_ffn_ref(x, router_w, router_b, expert_w, expert_b):
        import jax, jax.numpy as jnp
        import numpy as np
        B, N, D, C, E, K = (8, 4096, 64, 64, 8, 2)
        router_probs = jax.nn.softmax(x @ router_w + router_b, axis=-1)
        top_p, top_i = jax.lax.top_k(router_probs, K)
        top_p = top_p / jnp.sum(top_p, axis=-1, keepdims=True)
        expert_out = jnp.einsum('bnd,edc->bnec', x, expert_w) + expert_b
        gathered = jnp.take_along_axis(expert_out, top_i[..., None], axis=2)
        return jnp.einsum('bnk,bnkc->bnc', top_p, gathered)

    def _gn(v, G=32, eps=1e-05):
        B_, H_, W_, C_ = v.shape
        g = v.reshape(B_, H_, W_, G, C_ // G)
        m = jnp.mean(g, axis=(1, 2, 4), keepdims=True)
        s = jnp.var(g, axis=(1, 2, 4), keepdims=True)
        return ((g - m) / jnp.sqrt(s + eps)).reshape(v.shape)

    def _ln_c(v, eps=1e-06):
        m = jnp.mean(v, axis=-1, keepdims=True)
        s = jnp.var(v, axis=-1, keepdims=True)
        return (v - m) / jnp.sqrt(s + eps)

    def _ln_t(v, eps=1e-05):
        m = jnp.mean(v, axis=-1, keepdims=True)
        s = jnp.var(v, axis=-1, keepdims=True)
        return (v - m) / jnp.sqrt(s + eps)

    def _to_tokens(v):
        B_, H_, W_, C_ = v.shape
        return v.reshape(B_, H_ * W_, C_)

    def _from_tokens(t, like):
        return t.reshape(like.shape)
    x = x + _L0_conv_ref(_ln_c(x), L0_conv_mask, L0_conv_Wq, L0_conv_Wk, L0_conv_Wv, L0_conv_Wg, L0_conv_Wo, L0_conv_Wb)
    t = _to_tokens(x)
    t = t + _L0_ffn_ref(_ln_t(t), L0_ffn_router_w, L0_ffn_router_b, L0_ffn_expert_w, L0_ffn_expert_b)
    x = _from_tokens(t, x)
    return x

_drawn_inputs = setup_inputs


def setup_inputs(seed=0):
    import zlib

    import numpy as np

    out = dict(_drawn_inputs(seed))
    spreads = {'L0_ffn_router_b': (0.0, 0.1), 'L0_ffn_expert_b': (0.0, 0.1)}
    factors = {}
    for name, (base, spread) in spreads.items():
        noise = np.random.default_rng([zlib.crc32(name.encode()), seed]).standard_normal(out[name].shape)
        drawn = base * np.exp(spread * noise) if base else spread * noise
        out[name] = jnp.asarray(drawn.astype(out[name].dtype))
    for name, factor in factors.items():
        out[name] = (out[name] * factor).astype(out[name].dtype)
    return out
```

```python
from contextlib import ExitStack

import concourse.bass as bass
from concourse import mybir

ALU = mybir.AluOpType
ACT = mybir.ActivationFunctionType
AX = mybir.AxisListType
F32 = mybir.dt.float32
F16 = mybir.dt.float16

P = 128
N = 160
D = 64
H = 4
DH = 32
E = 8
RG = 4
TG = RG * N
T = TG // P
GROUPS = N // RG
REST = N - P
CH = TG // 2
NT = H + 1
UP = 16.0
SCALE = DH ** -0.5
EPS1, EPS2 = 1e-6, 1e-5
FAR = 1e30
ROOT_D = float(D) ** 0.5


def need(eng, sem, value):
    if isinstance(value, int) and value <= 0:
        return
    eng.wait_ge(sem, value)


def build(nc, x, WqT, WkT, Wv, Wg, Wo, Wb, router_w, router_b, expert_w, expert_b, mask, out):
    with ExitStack() as ctx:
        def sb(name, shape, dt=F32):
            return ctx.enter_context(nc.sbuf_tensor(name, shape, dt))

        def sem(name):
            return ctx.enter_context(nc.semaphore(name))

        ps_scores = [[ctx.enter_context(nc.psum_tensor(f"ps_scores{a}{b}", [P, 512], F32))
                      for b in range(2)] for a in range(2)]
        ps_y = ctx.enter_context(nc.psum_tensor("ps_y", [P, 512], F32))
        ps_pt = ctx.enter_context(nc.psum_tensor("ps_pt", [P, 512], F32))
        ps_o = ctx.enter_context(nc.psum_tensor("ps_o", [P, 512], F32))
        ps_m = ctx.enter_context(nc.psum_tensor("ps_m", [P, 512], F32))
        ps_m16 = ps_m[:].bitcast(F16)

        ident = sb("ident", [P, P])
        ident16 = sb("ident16", [P, P], F16)
        headmask = sb("headmask", [P, H])
        half = sb("half", [P, T])
        eps1, eps2 = sb("eps1", [P, T]), sb("eps2", [P, T])
        order = sb("order", [P, T, E])
        w_raw = sb("w_raw", [P, 844])
        w_up = sb("w_up", [P, 844])
        w_hi = sb("w_hi", [P, 844], F16)
        w_lo = sb("w_lo", [P, 844], F16)
        qk_raw = sb("qk_raw", [P, 2, P])
        g_up = sb("g_up", [P, H, P])
        g_hi = sb("g_hi", [P, H, P], F16)
        g_lo = sb("g_lo", [P, H, P], F16)
        rb = sb("rb", [P, T, E])
        eb_raw = sb("eb_raw", [P, T, D])
        eb_hi = sb("eb_hi", [P, T, D], F16)
        eb_diff = sb("eb_diff", [P, T, D])
        eb_sel = sb("eb_sel", [P, T, D], F16)
        is_lo = sb("is_lo", [P, 2])
        bias32 = sb("bias32", [P, NT, N])
        bias_hi = sb("bias_hi", [P, NT, N], F16)
        bias_lo = sb("bias_lo", [P, NT, N], F16)
        V0, G0, X0, R0, B0, O0 = 0, 128, 256, 768, 776, 780

        xin = [sb(f"xin{a}", [P, T, D]) for a in range(2)]
        ln_s = [sb(f"ln_s{a}", [P, 4, T]) for a in range(2)]
        xc = [sb(f"xc{a}", [P, T, D]) for a in range(2)]
        sq = [sb(f"sq{a}", [P, T, D]) for a in range(2)]
        xn = [sb(f"xn{a}", [P, T, D]) for a in range(2)]
        hl = [sb(f"hl{a}", [P, T, 2, D], F16) for a in range(2)]
        ln_v = [sb(f"ln_v{a}", [P, T]) for a in range(2)]
        xs_all = sb("xs_all", [P, GROUPS * TG], F16)
        wb = sb("wb", [P, 2, 32], F16)
        mask_u8 = sb("mask_u8", [P, N], mybir.dt.uint8)
        pen = sb("pen", [P, N])
        xs_mask = [sb(f"xs_mask{a}", [P, TG], F16) for a in range(2)]
        b_stage = [sb(f"b_stage{a}", [P, N]) for a in range(2)]
        xs = [sb(f"xs{a}", [P, TG], F16) for a in range(2)]
        y_hi = [sb(f"y_hi{c}", [P, H, CH], F16) for c in range(2)]
        y_lo = [sb(f"y_lo{c}", [P, H, CH], F16) for c in range(2)]
        v_main = [sb(f"v_main{a}", [P, RG, P]) for a in range(2)]
        v_bd = [sb(f"v_bd{a}", [P, RG, H, DH]) for a in range(2)]
        gate = [sb(f"gate{a}", [P, TG]) for a in range(2)]
        negmax = [sb(f"negmax{a}", [P, NT]) for a in range(2)]
        nbias = [sb(f"nbias{a}", [P, NT]) for a in range(2)]
        psum_row = [sb(f"psum_row{a}", [P, NT]) for a in range(2)]
        rinv = [sb(f"rinv{a}", [P, NT]) for a in range(2)]
        probs = [sb(f"probs{a}", [P, NT, N]) for a in range(2)]
        pn_main = [sb(f"pn_main{a}", [P, H, P]) for a in range(2)]
        pn_rest = [sb(f"pn_rest{a}", [P, H, REST]) for a in range(2)]
        pn_pack = [sb(f"pn_pack{a}", [P, N]) for a in range(2)]
        pt_main = [sb(f"pt_main{a}", [P, H, N]) for a in range(2)]
        pt_pack = [sb(f"pt_pack{a}", [P, N]) for a in range(2)]
        og = sb("og", [P, TG])
        og_hi = sb("og_hi", [P, TG], F16)
        og_lo = sb("og_lo", [P, TG], F16)
        x1 = [sb(f"x1_{a}", [P, T, D]) for a in range(2)]
        xs2 = sb("xs2", [P, T, P], F16)
        lg = sb("lg", [P, T, E])
        rt = sb("rt", [P, 8, T, E])
        rs = sb("rs", [P, 12, T])
        coef = sb("coef", [P, T, E])
        c_stack = sb("c_stack", [P, P], F16)
        c_t = sb("c_t", [P, P], F16)
        prod = [sb(f"prod{a}", [P, 8, D]) for a in range(2)]
        add1 = [sb(f"add1{a}", [P, 4, D]) for a in range(2)]
        add2 = [sb(f"add2{a}", [P, 2, D]) for a in range(2)]
        ymix = sb("ymix", [P, T, D])
        yall = sb("yall", [P, T, D])
        res = [sb(f"res{a}", [P, T, D]) for a in range(2)]

        b_dram = nc.dram_tensor("bias_scratch", [N, 32, N], F32, kind="Internal").ap()

        w_loaded, const_ready = sem("w_loaded"), sem("const_ready")
        wprep, gprod_done, w_ready = sem("wprep"), sem("gprod_done"), sem("w_ready")
        x_loaded = [sem(f"x_loaded{a}") for a in range(2)]
        sq_done, sq2_done = sem("sq_done"), sem("sq2_done")
        lnA, lnP, lnS, hi_ready, lo_ready = sem("lnA"), sem("lnP"), sem("lnS"), sem("hi_ready"), sem("lo_ready")
        t1_done, xs_made, b_done, b_evac = sem("t1_done"), sem("xs_made"), sem("b_done"), sem("b_evac")
        xs_kept = [sem(f"xs_kept{a}") for a in range(2)]
        b_written = [sem(f"b_written{a}") for a in range(2)]
        b_loaded, b_ready = sem("b_loaded"), sem("b_ready")
        xs_loaded = [sem(f"xs_loaded{a}") for a in range(2)]
        y_done, yhi_done, ylo_done = sem("y_done"), sem("yhi_done"), sem("ylo_done")
        s_done, max_done, nb_done, exp_done = sem("s_done"), sem("max_done"), sem("nb_done"), sem("exp_done")
        rinv_done, pnm_done, pnr_done, tr_done = sem("rinv_done"), sem("pnm_done"), sem("pnr_done"), sem("tr_done")
        alpha_done, beta_done, ptm_done, ptb_done = sem("alpha_done"), sem("beta_done"), sem("ptm_done"), sem("ptb_done")
        v_done, v_evac, vr_done, vr_evac = sem("v_done"), sem("v_evac"), sem("vr_done"), sem("vr_evac")
        g_done, g_evac = sem("g_done"), sem("g_evac")
        av_done, og_done, ogh_done, ogl_done = sem("av_done"), sem("og_done"), sem("ogh_done"), sem("ogl_done")
        wo_done, x1_done = sem("wo_done"), sem("x1_done")
        ln2A, ln2P, ln2S, hi2_ready, lo2_ready = sem("ln2A"), sem("ln2P"), sem("ln2S"), sem("hi2_ready"), sem("lo2_ready")
        t2_done, xs2_done = sem("t2_done"), sem("xs2_done")
        rt_done, lg_done, rt_step, rt_exp = sem("rt_done"), sem("lg_done"), sem("rt_step"), sem("rt_exp")
        c_ready, ct_done, ct_evac = sem("c_ready"), sem("ct_done"), sem("ct_evac")
        e_done, prod_done, mix_step, cb_done, yall_done, res_done = (
            sem("e_done"), sem("prod_done"), sem("mix_step"), sem("cb_done"), sem("yall_done"), sem("res_done"))
        res_stored = [sem(f"res_stored{a}") for a in range(2)]

        x_flat = x.rearrange("a r j d -> (a r j d)")
        out_flat = out.rearrange("a r j d -> (a r j d)")
        b_flat = b_dram.rearrange("r h j -> (r h j)")
        tokens = lambda flat, start: flat[bass.ds(start, TG * D)].rearrange("(p t d) -> p t d", p=P, t=T)
        KE = ctx.enter_context(nc.Block())

        def pairs_loop(eng, body, first, end):
            with eng.Fori(0, (end - first) // 2) as i:
                body(i * 2 + first, 0)
                body(i * 2 + (first + 1), 1)

        N_CONST = 16 + 1 + 2
        def run_phase1(eng, step):
            step(0, 0, 1, 0, 0)
            step(1, 1, 1, 1, 0)
            pairs_loop(eng, lambda n, a: step(n, a, 1, 1, 1), 2, GROUPS)
            step(GROUPS, 0, 0, 1, 1)
            step(GROUPS + 1, 1, 0, 0, 1)

        def run_steps(eng, step):
            step(0, 0, (1, 0, 0, 1))
            step(1, 1, (1, 1, 0, 1))
            pairs_loop(eng, lambda n, a: step(n, a, (1, 1, 1, 1)), 2, GROUPS - 2)
            step(GROUPS - 2, 0, (1, 1, 1, 1))
            step(GROUPS - 1, 1, (1, 1, 1, 0))
            step(GROUPS, 0, (0, 1, 1, 0))
            step(GROUPS + 1, 1, (0, 0, 1, 0))

        N_WLOAD = 2 * 5 + 3 + T + 3 * T + 1

        @KE.sync
        def _(sp):
            ld = lambda dst, src: sp.dma_start(dst, src).then_inc(w_loaded, 16)
            for half_ in range(2):
                rows = slice(64 * half_, 64 * half_ + 64)
                ld(w_raw[rows, V0:V0 + 128], Wv)
                ld(w_raw[rows, G0:G0 + 128], Wg)
                ld(w_raw[rows, X0:X0 + 512].rearrange("p (e c) -> p e c", e=E), expert_w.rearrange("e d c -> d e c"))
                ld(w_raw[rows, R0:R0 + 8], router_w)
                ld(w_raw[rows, B0:B0 + 4], Wb)
            ld(w_raw[:, O0:O0 + 64], Wo)
            ld(qk_raw[:, 0, :], WqT)
            ld(qk_raw[:, 1, :], WkT)
            for t in range(T):
                ld(rb[:, t, :], router_b.rearrange("(a e) -> a e", a=1).broadcast_to([P, E]))
            ld(mask_u8[D:P, :], mask.broadcast_to([P - D, N]))
            sp.wait_ge(const_ready, 1)
            for t in range(T):
                for part in range(3):
                    ld(eb_raw[40 * part + 8 * t:40 * part + 8 * t + 8, t, :], expert_b)

            def at(g, size):
                return g * size if isinstance(g, int) else sp.snap(g * size)

            def load_x(g, a):
                start = at(g, TG * D)
                need(sp, lnA, 3 * g - 3)
                sp.dma_start(xin[a][:], tokens(x_flat, start)).then_inc(x_loaded[a], 16)

            def keep_xs(g, a):
                start = at(g, TG)
                sp.wait_ge(xs_made, g + 1)
                sp.dma_start(xs_all[:, bass.ds(start, TG)], xs[a][:]).then_inc(xs_kept[a], 16)

            def store_bias(g, a):
                start = at(g, P * N)
                sp.wait_ge(b_evac, g + 1)
                sp.dma_start(b_flat[bass.ds(start, P * N)].rearrange("(r j) -> r j", j=N), b_stage[a][:]).then_inc(b_written[a], 16)

            for g in range(2):
                load_x(g, g)

            def phase1(g, a):
                load_x(g + 2, a)
                keep_xs(g, a)
                store_bias(g, a)

            pairs_loop(sp, phase1, 0, GROUPS - 2)
            for a in range(2):
                keep_xs(GROUPS - 2 + a, a)
                store_bias(GROUPS - 2 + a, a)
            for a in range(2):
                sp.wait_ge(b_written[a], 16 * (GROUPS // 2))
            sp.dma_start(bias32[:, 0:H, :], b_dram[0:P, 0:H, :]).then_inc(b_loaded, 16)
            for h in range(H):
                sp.dma_start(bias32[32 * h:32 * h + 32, H, :], b_dram[P:N, h, :]).then_inc(b_loaded, 16)

            def load_xs(g, a):
                start = at(g, TG)
                need(sp, s_done, 8 * (g - 1))
                sp.dma_start(xs[a][:], xs_all[:, bass.ds(start, TG)]).then_inc(xs_loaded[a], 16)
                sp.dma_start(xs_mask[a][0:D, :], xs_all[0:D, bass.ds(start, TG)]).then_inc(xs_loaded[a], 16)

            def load_res(g, a):
                start = at(g, TG * D)
                need(sp, x1_done, g - 1)
                sp.dma_start(xin[a][:], tokens(x_flat, start)).then_inc(x_loaded[a], 16)

            def store(g, a):
                start = at(g, TG * D)
                sp.wait_ge(res_done, g + 1)
                sp.dma_start(tokens(out_flat, start), res[a][:]).then_inc(res_stored[a], 16)

            for a in range(2):
                sp.wait_ge(xs_kept[a], 16 * (GROUPS // 2))
            for g in range(2):
                load_xs(g, g)
                load_res(g, g)

            def phase2(g, a):
                load_xs(g, a)
                load_res(g, a)
                store(g - 4, a)

            for g in range(2, 4):
                load_xs(g, g % 2)
                load_res(g, g % 2)
            pairs_loop(sp, phase2, 4, GROUPS)
            for g in range(GROUPS - 4, GROUPS):
                store(g, g % 2)
            for a in range(2):
                sp.wait_ge(res_stored[a], 16 * (GROUPS // 2))

        @KE.gpsimd
        def _(pool):
            pool.memset(eb_raw[:], 0.0).then_inc(const_ready, 1)
            pool.memset(ident[:], 0.0).then_inc(const_ready, 1)
            pool.memset(headmask[:], 0.0).then_inc(const_ready, 1)
            pool.memset(half[:], -0.5).then_inc(const_ready, 1)
            pool.memset(eps1[:], D * EPS1).then_inc(const_ready, 1)
            pool.memset(eps2[:], D * EPS2).then_inc(const_ready, 1)
            pool.memset(c_stack[:], 0.0).then_inc(const_ready, 1)
            pool.memset(is_lo[:], 0.0).then_inc(const_ready, 1)
            for e in range(E):
                pool.memset(order[:, :, e], float(E - e)).then_inc(const_ready, 1)
            pool.wait_ge(const_ready, 16)
            pool.affine_select(out=ident[:], in_=ident[:], compare_op=ALU.not_equal, fill=1.0, base=0,
                               pattern=[[-1, P]], channel_multiplier=1).then_inc(const_ready, 1)
            pool.affine_select(out=is_lo[:, 0:1], in_=is_lo[:, 0:1], compare_op=ALU.is_gt, fill=1.0, base=80,
                               pattern=[[0, 1]], channel_multiplier=-1).then_inc(const_ready, 1)
            pool.affine_select(out=is_lo[:, 1:2], in_=is_lo[:, 1:2], compare_op=ALU.is_ge, fill=1.0, base=-80,
                               pattern=[[0, 1]], channel_multiplier=1).then_inc(const_ready, 1)

            def ln_scale(g, a, sums, step, eps, own):
                pool.wait_ge(sums, g + 1)
                pool.tensor_tensor(ln_v[a][:], ln_s[a][:, 2, :], eps[:], ALU.add).then_inc(own, 1)
                pool.wait_ge(own, 3 * g + 1)
                pool.tensor_tensor(ln_s[a][:, 3, :], ln_v[a][:], half[:], ALU.pow).then_inc(own, 1)
                pool.wait_ge(own, 3 * g + 2)
                need(pool, step, g - 1)
                pool.tensor_tensor(xn[a][:], xc[a][:], ln_s[a][:, 3, :].unsqueeze(2).broadcast_to([P, T, D]),
                                   ALU.mult).then_inc(own, 1)

            def phase1(n, a, g0, g1, g2):
                if g1: ln_scale(n - 1, 1 - a, lnS, lo_ready, eps1, lnP)

            run_phase1(pool, phase1)

            def norm_main(g, r):
                a = r % 2
                pool.wait_ge(rinv_done, 4 * g + r + 1)
                need(pool, beta_done, 4 * g + r - 1)
                pool.tensor_tensor(pn_main[a][:], probs[a][:, 0:H, 0:P],
                                   rinv[a][:, 0:H].unsqueeze(2).broadcast_to([P, H, P]), ALU.mult).then_inc(pnm_done, 1)

            def og_low(g, r):
                pool.wait_ge(ogh_done, 4 * g + r + 1)
                pool.tensor_tensor(og_lo[:, N * r:N * r + N], og[:, N * r:N * r + N], og_hi[:, N * r:N * r + N],
                                   ALU.subtract).then_inc(ogl_done, 1)

            def mix(g, t):
                a, b = t % 2, 15 * g + 3 * t
                pool.wait_ge(prod_done, 5 * g + t + 1)
                pool.tensor_tensor(add1[a][:], prod[a][:, 0:4, :], prod[a][:, 4:8, :], ALU.add).then_inc(mix_step, 1)
                pool.wait_ge(mix_step, b + 1)
                pool.tensor_tensor(add2[a][:], add1[a][:, 0:2, :], add1[a][:, 2:4, :], ALU.add).then_inc(mix_step, 1)
                pool.wait_ge(mix_step, b + 2)
                if t == 0:
                    need(pool, yall_done, g)
                pool.tensor_tensor(ymix[:, t, :], add2[a][:, 0, :], add2[a][:, 1, :], ALU.add).then_inc(mix_step, 1)

            def step(n, a, do):
                att, wo, ex, _ = do
                if wo: norm_main(n - 1, 3)
                if wo: og_low(n - 1, 2)
                if att: norm_main(n, 0)
                if wo: og_low(n - 1, 3)
                if att: norm_main(n, 1)
                if ex: mix(n - 2, 0)
                if ex: mix(n - 2, 1)
                if att: og_low(n, 0)
                if att: norm_main(n, 2)
                if ex: mix(n - 2, 2)
                if ex: mix(n - 2, 3)
                if ex: mix(n - 2, 4)
                if wo: ln_scale(n - 1, (a + 1) % 2, ln2S, lo2_ready, eps2, ln2P)
                if att: og_low(n, 1)

            run_steps(pool, step)


        @KE.scalar
        def _(act):
            def square(g, a, src_done, sums, own):
                act.wait_ge(src_done, 3 * g + 3)
                need(act, sums, g - 1)
                act.activation(sq[a][:], xc[a][:], ACT.Square).then_inc(own, 1)

            def high(g, a, scaled, transposed, before, own):
                act.wait_ge(scaled, 3 * g + 3)
                need(act, transposed, before)
                act.activation(hl[a][:, :, 0, :], xn[a][:], ACT.Copy, scale=ROOT_D).then_inc(own, 1)

            def make_xs(g, a):
                act.wait_ge(t1_done, g + 1)
                need(act, b_done, g)
                need(act, xs_kept[a], 8 * g - 8 * a)
                act.activation(xs[a][:].rearrange("c (p t) -> c t p", t=T),
                               ps_m16[:, 0:TG].rearrange("c (t p) -> c t p", t=T), ACT.Copy).then_inc(xs_made, 1)

            def phase1(n, a, g0, g1, g2):
                if g0: square(n, a, lnA, lnS, sq_done)
                if g2: make_xs(n - 2, a)
                if g1: high(n - 1, 1 - a, lnP, t1_done, n - 2, hi_ready)

            run_phase1(act, phase1)

            def exp(n, r, u):
                a, k0, k1 = r % 2, (0, 3)[u], (3, NT)[u]
                act.wait_ge(nb_done, 8 * n + 2 * r + u + 1)
                need(act, pnm_done, 4 * n + r - 1)
                need(act, pnr_done, 2 * (4 * n + r - 1))
                for k in range(k0, k1):
                    e = act.activation(probs[a][:, k, :], ps_scores[a][u][:, (k - k0) * N:(k - k0 + 1) * N], ACT.Exp,
                                       bias=nbias[a][:, k:k + 1], scale=1.0 / UP, accum_out=psum_row[a][:, k:k + 1])
                e.then_inc(exp_done, 1)

            def pt_alpha(n, r):
                q, a = 4 * n + r, r % 2
                act.wait_ge(alpha_done, q + 1)
                need(act, av_done, q - 1)
                act.activation(pt_main[a][:, :, 0:P], ps_pt[:].rearrange("j (h i) -> j h i", h=H),
                               ACT.Copy).then_inc(ptm_done, 1)

            def pt_beta(n, r):
                q, a = 4 * n + r, r % 2
                act.wait_ge(beta_done, q + 1)
                act.activation(pt_main[a][:, :, P:N], ps_o[:, N:N + P].rearrange("j (h i) -> j h i", h=H),
                               ACT.Copy).then_inc(ptb_done, 1)
                act.activation(pt_pack[a][:, 0:P], ps_o[:, N + P:N + 2 * P], ACT.Copy).then_inc(ptb_done, 1)

            def y_high(g, c, h):
                act.wait_ge(y_done, 8 * g + 4 * c + h + 1)
                need(act, s_done, 8 * (g - 1) + 4 * (c + 1))
                act.activation(y_hi[c][:, h, :], ps_y[:, 0:CH], ACT.Copy).then_inc(yhi_done, 1)

            def og_high(n, r):
                act.wait_ge(og_done, 4 * n + r + 1)
                need(act, wo_done, n)
                act.activation(og_hi[:, N * r:N * r + N], og[:, N * r:N * r + N], ACT.Copy).then_inc(ogh_done, 1)

            def keep_v(n, a):
                act.wait_ge(v_done, n + 1)
                need(act, av_done, 4 * (n - 1))
                act.activation(v_main[a][:], ps_m[:].rearrange("j (r e) -> j r e", r=RG), ACT.Copy,
                               scale=1.0 / UP).then_inc(v_evac, 1)

            def tanh_gate(n, a, c):
                act.wait_ge(g_done, 2 * n + c + 1)
                need(act, og_done, 4 * (n - 1))
                act.activation(gate[a][:, CH * c:CH * c + CH], ps_m[:, 0:CH], ACT.Tanh,
                               scale=0.5 / UP).then_inc(g_evac, 1)

            def step(n, a, do):
                att, wo, ex, more = do
                b = 1 - a
                if att: keep_v(n, a)
                if att: exp(n, 0, 0)
                if att: exp(n, 0, 1)
                if wo: pt_alpha(n - 1, 3)
                if att: y_high(n, 1, 0)
                if wo: pt_beta(n - 1, 3)
                if att: tanh_gate(n, a, 0)
                if ex: high(n - 2, a, ln2P, t2_done, n - 2, hi2_ready)
                if wo: og_high(n - 1, 2)
                if att: y_high(n, 1, 1)
                if att: tanh_gate(n, a, 1)
                if ex:
                    act.wait_ge(t2_done, n - 1)
                    if not isinstance(n, int) or n > 2:
                        act.wait_ge(e_done, 5 * (n - 2))
                    act.activation(xs2[:], ps_m16[:, 0:TG].rearrange("c (t p) -> c t p", t=T), ACT.Copy).then_inc(xs2_done, 1)
                if att: exp(n, 1, 0)
                if att: exp(n, 1, 1)
                if att: pt_alpha(n, 0)
                if att: y_high(n, 1, 2)
                if att: pt_beta(n, 0)
                if wo: og_high(n - 1, 3)
                if att: y_high(n, 1, 3)
                if att: exp(n, 2, 0)
                if att: exp(n, 2, 1)
                if att: pt_alpha(n, 1)
                if more: y_high(n + 1, 0, 0)
                if att: pt_beta(n, 1)
                if ex:
                    act.wait_ge(rt_step, 21 * (n - 2) + 12)
                    act.activation(rs[:, 5, :], rs[:, 4, :], ACT.Exp, scale=1.0 / UP).then_inc(rt_exp, 1)
                if att: og_high(n, 0)
                if more: y_high(n + 1, 0, 1)
                if ex:
                    act.wait_ge(ct_done, n - 1)
                    act.activation(c_t[:], ps_m16[:, 0:P], ACT.Copy).then_inc(ct_evac, 1)
                if att: exp(n, 3, 0)
                if wo: square(n - 1, b, ln2A, ln2S, sq2_done)
                if att: exp(n, 3, 1)
                if att: pt_alpha(n, 2)
                if more: y_high(n + 1, 0, 2)
                if att: pt_beta(n, 2)
                if att: og_high(n, 1)
                if more: y_high(n + 1, 0, 3)

            for h in range(H):
                y_high(0, 0, h)
            run_steps(act, step)

        @KE.vector
        def _(dve):
            made = [0]

            def prep(ins):
                ins.then_inc(wprep, 1)
                made[0] += 1
                dve.wait_ge(wprep, made[0])

            dve.wait_ge(const_ready, N_CONST)
            dve.wait_ge(w_loaded, 16 * N_WLOAD)
            prep(dve.tensor_copy(ident16[:], ident[:]))
            for h in range(H):
                prep(dve.memset(headmask[32 * h:32 * h + 32, h:h + 1], 1.0 / UP))
            prep(dve.tensor_scalar(w_up[:], w_raw[:], UP, None, ALU.mult))
            prep(dve.tensor_copy(w_hi[:], w_up[:]))
            prep(dve.tensor_tensor(w_lo[:], w_up[:], w_hi[:], ALU.subtract))
            prep(dve.memset(wb[:], 0.0))
            prep(dve.tensor_copy(wb[:, 0, 0:H], w_hi[:, B0:B0 + H]))
            prep(dve.tensor_copy(wb[:, 1, 0:H], w_lo[:, B0:B0 + H]))
            dve.wait_ge(gprod_done, 1)
            for h in range(H):
                prep(dve.tensor_scalar(g_up[:, h, :], ps_scores[h // 2][h % 2][:, 0:P], SCALE * UP, None, ALU.mult))
            prep(dve.tensor_copy(g_hi[:], g_up[:]))
            prep(dve.tensor_tensor(g_lo[:], g_up[:], g_hi[:], ALU.subtract))
            prep(dve.tensor_scalar(rb[:], rb[:], UP, None, ALU.mult))
            prep(dve.tensor_scalar(eb_raw[:], eb_raw[:], UP, None, ALU.mult))
            prep(dve.tensor_copy(eb_hi[:], eb_raw[:]))
            prep(dve.tensor_tensor(eb_diff[:], eb_raw[:], eb_hi[:], ALU.subtract))
            prep(dve.tensor_scalar(eb_diff[:], eb_diff[:], is_lo[:, 0:1], None, ALU.mult))
            prep(dve.scalar_tensor_tensor(out=eb_sel[:], in0=eb_hi[:], scalar=is_lo[:, 1:2], in1=eb_diff[:],
                                          op0=ALU.mult, op1=ALU.add))
            prep(dve.tensor_scalar(pen[D:P, :], mask_u8[D:P, :], -1.0, 65504.0, ALU.add, ALU.mult))
            for a in range(2):
                for r in range(RG):
                    prep(dve.tensor_copy(xs_mask[a][D:P, N * r:N * r + N], pen[D:P, :]))
                prep(dve.memset(y_lo[a][D:P, :, :], 32768.0))
            dve.nop().then_inc(w_ready, 1)

            def center(g, a, src, own, used_by_square, used_by_scale):
                dve.tensor_reduce(ln_s[a][:, 0, :], src[a][:], AX.X, ALU.add).then_inc(own, 1)
                dve.wait_ge(own, 3 * g + 1)
                dve.tensor_scalar(ln_s[a][:, 1, :], ln_s[a][:, 0, :], -1.0 / D, None, ALU.mult).then_inc(own, 1)
                dve.wait_ge(own, 3 * g + 2)
                need(dve, used_by_square, g - 1)
                need(dve, used_by_scale, 3 * (g - 1))
                dve.tensor_tensor(xc[a][:], src[a][:], ln_s[a][:, 1, :].unsqueeze(2).broadcast_to([P, T, D]),
                                  ALU.add).then_inc(own, 1)

            def sum_squares(g, a, squared, scaled, own):
                dve.wait_ge(squared, g + 1)
                need(dve, scaled, 3 * (g - 1))
                dve.tensor_reduce(ln_s[a][:, 2, :], sq[a][:], AX.X, ALU.add).then_inc(own, 1)

            def low(g, a, high_done, own):
                dve.wait_ge(high_done, g + 1)
                dve.scalar_tensor_tensor(out=hl[a][:, :, 1, :], in0=xn[a][:], scalar=ROOT_D, in1=hl[a][:, :, 0, :],
                                         op0=ALU.mult, op1=ALU.subtract).then_inc(own, 1)

            def phase1(n, a, g0, g1, g2):
                if g2: low(n - 2, a, hi_ready, lo_ready)
                if g1: sum_squares(n - 1, 1 - a, sq_done, lnP, lnS)
                if g0:
                    dve.wait_ge(x_loaded[a], 8 * n + 16 - 8 * a)
                    center(n, a, xin, lnA, sq_done, lnP)
                if g2:
                    dve.wait_ge(b_done, n - 1)
                    need(dve, b_written[a], 8 * (n - 2) - 8 * a)
                    dve.tensor_copy(b_stage[a][:], ps_y[:, 0:N]).then_inc(b_evac, 1)

            run_phase1(dve, phase1)
            dve.wait_ge(b_loaded, 16 * 5)
            prep(dve.tensor_copy(bias_hi[:], bias32[:]))
            dve.tensor_tensor(bias_lo[:], bias32[:], bias_hi[:], ALU.subtract).then_inc(b_ready, 1)

            def row_max(n, r, u):
                a, k0, k1 = r % 2, (0, 3)[u], (3, NT)[u]
                i = 8 * n + 2 * r + u
                dve.wait_ge(s_done, i + 1)
                dve.tensor_reduce(negmax[a][:, k0:k1],
                                  ps_scores[a][u][:, 0:(k1 - k0) * N].rearrange("i (k j) -> i k j", j=N),
                                  AX.X, ALU.max, negate=True).then_inc(max_done, 1)
                dve.wait_ge(max_done, i + 1)
                dve.tensor_scalar(nbias[a][:, k0:k1], negmax[a][:, k0:k1], 1.0 / UP, None, ALU.mult).then_inc(nb_done, 1)

            def norm_rest(n, r):
                q, a = 4 * n + r, r % 2
                dve.wait_ge(exp_done, 2 * q + 2)
                need(dve, pnm_done, q - 1)
                dve.reciprocal(rinv[a][:], psum_row[a][:]).then_inc(rinv_done, 1)
                dve.wait_ge(rinv_done, q + 1)
                need(dve, beta_done, q - 1)
                dve.tensor_scalar(pn_pack[a][:], probs[a][:, H, :], rinv[a][:, H:NT], None, ALU.mult).then_inc(pnr_done, 1)
                dve.tensor_tensor(pn_rest[a][:], probs[a][:, 0:H, P:N],
                                  rinv[a][:, 0:H].unsqueeze(2).broadcast_to([P, H, REST]), ALU.mult).then_inc(pnr_done, 1)
                dve.wait_ge(pnr_done, 2 * q + 1)
                need(dve, av_done, q - 1)
                dve.transpose(pt_pack[a][:, P:N], pn_pack[a][:, P:N]).then_inc(tr_done, 1)

            def y_low(g, c, h):
                i = 8 * g + 4 * c + h
                dve.wait_ge(yhi_done, i + 1)
                dve.tensor_tensor(y_lo[c][0:D, h, :], ps_y[0:D, 0:CH], y_hi[c][0:D, h, :], ALU.subtract).then_inc(ylo_done, 1)

            def gated(n, r, a):
                q = 4 * n + r
                dve.wait_ge(av_done, q + 1)
                dve.wait_ge(g_evac, 2 * n + 2)
                need(dve, ogl_done, q - 3)
                dve.scalar_tensor_tensor(out=og[:, N * r:N * r + N], in0=gate[a][:, N * r:N * r + N], scalar=1.0,
                                         in1=ps_o[:, 0:N], op0=ALU.add, op1=ALU.mult).then_inc(og_done, 1)

            def keep_v_rest(n, a):
                dve.wait_ge(vr_done, n + 1)
                need(dve, av_done, 4 * (n - 1))
                dve.tensor_tensor(v_bd[a][:],
                                  ps_m[:, 0:RG * DH].rearrange("j (r e) -> j r e", r=RG).unsqueeze(2).broadcast_to([P, RG, H, DH]),
                                  headmask[:].unsqueeze(1).unsqueeze(3).broadcast_to([P, RG, H, DH]),
                                  ALU.mult).then_inc(vr_evac, 1)

            def attention_out(g, a):
                dve.wait_ge(wo_done, g + 1)
                dve.wait_ge(x_loaded[a], 8 * GROUPS + 8 * g + 16 - 8 * a)
                need(dve, res_done, g - 1)
                dve.scalar_tensor_tensor(out=x1[a][:], in0=ps_m[:, 0:T * D].rearrange("p (t d) -> p t d", t=T),
                                         scalar=0.5 / UP, in1=xin[a][:], op0=ALU.mult, op1=ALU.add).then_inc(x1_done, 1)
                dve.wait_ge(x1_done, g + 1)
                center(g, a, x1, ln2A, sq2_done, ln2P)

            wide = lambda v: v.unsqueeze(2).broadcast_to([P, T, E])

            def route(g, part):
                def then(ins, k):
                    ins.then_inc(rt_step, 1)
                    dve.wait_ge(rt_step, 21 * g + k)

                L, tt, red = lg[:], dve.tensor_tensor, dve.tensor_reduce
                if part == 0:
                    dve.wait_ge(rt_done, g + 1)
                    tt(L, ps_m[:, 0:T * E].rearrange("p (t e) -> p t e", t=T), rb[:], ALU.add).then_inc(lg_done, 1)
                    dve.wait_ge(lg_done, g + 1)
                    then(red(rs[:, 0, :], L, AX.X, ALU.max), 1)
                    then(tt(rt[:, 0], L, wide(rs[:, 0, :]), ALU.is_equal), 2)
                    then(tt(rt[:, 1], rt[:, 0], order[:], ALU.mult), 3)
                    then(red(rs[:, 1, :], rt[:, 1], AX.X, ALU.max), 4)
                    then(tt(rt[:, 2], rt[:, 1], wide(rs[:, 1, :]), ALU.is_equal), 5)
                if part == 1:
                    then(dve.scalar_tensor_tensor(out=rt[:, 3], in0=rt[:, 2], scalar=-FAR, in1=L, op0=ALU.mult, op1=ALU.add), 6)
                    then(red(rs[:, 2, :], rt[:, 3], AX.X, ALU.max), 7)
                    then(tt(rt[:, 4], rt[:, 3], wide(rs[:, 2, :]), ALU.is_equal), 8)
                    then(tt(rt[:, 5], rt[:, 4], order[:], ALU.mult), 9)
                    then(red(rs[:, 3, :], rt[:, 5], AX.X, ALU.max), 10)
                    then(tt(rt[:, 6], rt[:, 5], wide(rs[:, 3, :]), ALU.is_equal), 11)
                    then(tt(rs[:, 4, :], rs[:, 2, :], rs[:, 0, :], ALU.subtract), 12)
                if part == 2:
                    dve.wait_ge(rt_exp, g + 1)
                    then(dve.tensor_scalar(rs[:, 6, :], rs[:, 5, :], 1.0, None, ALU.add), 13)
                    then(dve.reciprocal(rs[:, 7, :], rs[:, 6, :]), 14)
                    then(tt(rs[:, 8, :], rs[:, 5, :], rs[:, 7, :], ALU.mult), 15)
                    then(tt(rt[:, 7], rt[:, 2], wide(rs[:, 7, :]), ALU.mult), 16)
                    then(tt(rt[:, 0], rt[:, 6], wide(rs[:, 8, :]), ALU.mult), 17)
                    then(tt(coef[:], rt[:, 7], rt[:, 0], ALU.add), 18)
                    flat = coef[:].rearrange("p t e -> p (t e)")
                    then(dve.tensor_copy(c_stack[:, 0:40], flat), 19)
                    then(tt(c_stack[:, 40:80], flat, c_stack[:, 0:40], ALU.subtract), 20)
                    then(dve.tensor_copy(c_stack[:, 80:120], c_stack[:, 0:40]), 21)

            def weigh(g, t):
                a = t % 2
                dve.wait_ge(e_done, 5 * g + t + 1)
                if t >= 2:
                    dve.wait_ge(mix_step, 15 * g + 3 * (t - 2) + 1)
                dve.tensor_tensor(prod[a][:], ps_m[:].rearrange("p (e c) -> p e c", e=E),
                                  coef[:, t, :].unsqueeze(2).broadcast_to([P, E, D]), ALU.mult).then_inc(prod_done, 1)

            def finish(g, a):
                dve.wait_ge(cb_done, g + 1)
                dve.wait_ge(mix_step, 15 * g + 15)
                dve.tensor_tensor(yall[:], ps_m[:, 0:T * D].rearrange("p (t d) -> p t d", t=T), ymix[:], ALU.add).then_inc(yall_done, 1)
                dve.wait_ge(yall_done, g + 1)
                need(dve, res_stored[a], 8 * g - 8 * a)
                dve.scalar_tensor_tensor(out=res[a][:], in0=yall[:], scalar=1.0 / UP, in1=x1[a][:],
                                         op0=ALU.mult, op1=ALU.add).then_inc(res_done, 1)

            def step(n, a, do):
                att, wo, ex, more = do
                b = 1 - a
                if att: row_max(n, 0, 0)
                if att: row_max(n, 0, 1)
                if att: keep_v_rest(n, a)
                if att: y_low(n, 1, 0)
                if ex: low(n - 2, a, hi2_ready, lo2_ready)
                if wo: gated(n - 1, 2, b)
                if att: y_low(n, 1, 1)
                if att: norm_rest(n, 0)
                if att: row_max(n, 1, 0)
                if att: row_max(n, 1, 1)
                if att: y_low(n, 1, 2)
                if ex: route(n - 2, 0)
                if wo: gated(n - 1, 3, b)
                if att: y_low(n, 1, 3)
                if att: norm_rest(n, 1)
                if att: row_max(n, 2, 0)
                if ex: route(n - 2, 1)
                if att: row_max(n, 2, 1)
                if wo: attention_out(n - 1, b)
                if more: y_low(n + 1, 0, 0)
                if ex: route(n - 2, 2)
                if ex: weigh(n - 2, 0)
                if att: gated(n, 0, a)
                if more: y_low(n + 1, 0, 1)
                if ex: weigh(n - 2, 1)
                if att: norm_rest(n, 2)
                if att: row_max(n, 3, 0)
                if att: row_max(n, 3, 1)
                if ex: weigh(n - 2, 2)
                if wo: sum_squares(n - 1, b, sq2_done, ln2P, ln2S)
                if more: y_low(n + 1, 0, 2)
                if ex: weigh(n - 2, 3)
                if att: gated(n, 1, a)
                if more: y_low(n + 1, 0, 3)
                if ex: weigh(n - 2, 4)
                if att: norm_rest(n, 3)
                if ex: finish(n - 2, a)

            for h in range(H):
                y_low(0, 0, h)
            run_steps(dve, step)

        @KE.tensor
        def _(pe):
            mm = pe.matmul
            pe.wait_ge(const_ready, N_CONST)
            pe.wait_ge(w_loaded, 16 * N_WLOAD)
            for h in range(H):
                last = mm(ps_scores[h // 2][h % 2][:, 0:P], lhsT=qk_raw[32 * h:32 * h + 32, 0, :],
                          rhs=qk_raw[32 * h:32 * h + 32, 1, :], start=True, stop=True)
            last.then_inc(gprod_done, 1)
            pe.wait_ge(w_ready, 1)

            def turn(g, a, split, done):
                pe.wait_ge(split, g + 1)
                for t in range(T):
                    last = pe.transpose(ps_m16[:, P * t:P * t + P], hl[a][:, t, :, :].rearrange("p s d -> p (s d)"), ident16[:])
                last.then_inc(done, 1)

            def bias_of(g, a):
                need(pe, b_evac, g)
                pe.wait_ge(xs_made, g + 1)
                for r in range(RG):
                    cols = xs[a][:, N * r:N * r + N]
                    mm(ps_y[32 * r:32 * r + 32, 0:N], lhsT=wb[:, 0, :], rhs=cols, start=True, stop=False)
                    last = mm(ps_y[32 * r:32 * r + 32, 0:N], lhsT=wb[:, 1, :], rhs=cols, start=False, stop=True)
                last.then_inc(b_done, 1)

            def phase1(n, a, g0, g1, g2):
                if g2:
                    need(pe, xs_made, n - 2)
                    turn(n - 2, a, lo_ready, t1_done)
                    bias_of(n - 2, a)

            run_phase1(pe, phase1)

            def y_of(g, c, h, a):
                i = 8 * g + 4 * c + h
                if c == 0 and h == 0:
                    pe.wait_ge(xs_loaded[a], 16 * g + 32 - 16 * a)
                need(pe, ylo_done, i)
                cols = xs[a][:, CH * c:CH * c + CH]
                mm(ps_y[:, 0:CH], lhsT=g_hi[:, h, :], rhs=cols, start=True, stop=False)
                mm(ps_y[:, 0:CH], lhsT=g_lo[:, h, :], rhs=cols, start=False, stop=True).then_inc(y_done, 1)

            def scores(n, r, u, a):
                q, c, off = 4 * n + r, r // 2, (r % 2) * N
                pe.wait_ge(ylo_done, 8 * n + 4 * c + 4)
                need(pe, exp_done, 2 * q + u + 1 - 4)
                full, part = xs[a][:, N * r:N * r + N], xs_mask[a][:, N * r:N * r + N]
                for k in ((0, 1, 2), (3,))[u]:
                    o = ps_scores[r % 2][u][:, (k % 3) * N:(k % 3) * N + N]
                    mm(o, lhsT=y_hi[c][:, k, off:off + P], rhs=full, start=True, stop=False)
                    mm(o, lhsT=y_lo[c][:, k, off:off + P], rhs=part, start=False, stop=False)
                    mm(o, lhsT=ident16[:], rhs=bias_hi[:, k, :], start=False, stop=False)
                    last = mm(o, lhsT=ident16[:], rhs=bias_lo[:, k, :], start=False, stop=True)
                if u == 1:
                    for h in range(H):
                        o = ps_scores[r % 2][1][32 * h:32 * h + 32, N:2 * N]
                        mm(o, lhsT=y_hi[c][:, h, off + P:off + N], rhs=full, start=True, stop=False)
                        mm(o, lhsT=y_lo[c][:, h, off + P:off + N], rhs=part, start=False, stop=False)
                    o = ps_scores[r % 2][1][:, N:2 * N]
                    mm(o, lhsT=ident16[:], rhs=bias_hi[:, H, :], start=False, stop=False)
                    last = mm(o, lhsT=ident16[:], rhs=bias_lo[:, H, :], start=False, stop=True)
                last.then_inc(s_done, 1)

            def alpha(n, r):
                q, a = 4 * n + r, r % 2
                pe.wait_ge(pnm_done, q + 1)
                need(pe, ptm_done, q)
                for h in range(H):
                    last = pe.transpose(ps_pt[:, P * h:P * h + P], pn_main[a][:, h, :], ident[:])
                last.then_inc(alpha_done, 1)

            def beta(n, r):
                q, a = 4 * n + r, r % 2
                pe.wait_ge(pnr_done, 2 * q + 2)
                need(pe, og_done, q - 1)
                pe.transpose(ps_o[:, N:N + P], pn_pack[a][:, 0:P], ident[:])
                pe.transpose(ps_o[:, N + P:N + 2 * P], pn_rest[a][:].rearrange("i h j -> i (h j)"), ident[:]).then_inc(beta_done, 1)

            def attend(n, r, a):
                q, b = 4 * n + r, r % 2
                pe.wait_ge(ptm_done, q + 1)
                pe.wait_ge(tr_done, q + 1)
                if more_beta[0]:
                    pe.wait_ge(ptb_done, 2 * q + 4)
                else:
                    pe.wait_ge(ptb_done, 2 * q + 2)
                pe.wait_ge(v_evac, n + 1)
                pe.wait_ge(vr_evac, n + 1)
                need(pe, og_done, q)
                for h in range(H):
                    mm(ps_o[32 * h:32 * h + 32, 0:N], lhsT=v_main[a][:, r, 32 * h:32 * h + 32], rhs=pt_main[b][:, h, :],
                       start=True, stop=False)
                mm(ps_o[:, 0:N], lhsT=v_bd[a][:, r].rearrange("j h e -> j (h e)"), rhs=pt_pack[b][:], start=False, stop=True).then_inc(av_done, 1)

            more_beta = [True]

            def project_v(n, a):
                need(pe, x1_done, n - 1)
                need(pe, yall_done, n - 2)
                for r in range(RG):
                    cols = xs[a][:, N * r:N * r + P]
                    mm(ps_m[:, P * r:P * r + P], lhsT=cols, rhs=w_hi[:, V0:V0 + P], start=True, stop=False)
                    last = mm(ps_m[:, P * r:P * r + P], lhsT=cols, rhs=w_lo[:, V0:V0 + P], start=False, stop=True)
                last.then_inc(v_done, 1)

            def project_v_rest(n, a):
                pe.wait_ge(v_evac, n + 1)
                for r in range(RG):
                    cols = xs[a][:, N * r + P:N * r + N]
                    for h in range(H):
                        o = ps_m[32 * h:32 * h + 32, DH * r:DH * r + DH]
                        mm(o, lhsT=cols, rhs=w_hi[:, V0 + DH * h:V0 + DH * h + DH], start=True, stop=False)
                        last = mm(o, lhsT=cols, rhs=w_lo[:, V0 + DH * h:V0 + DH * h + DH], start=False, stop=True)
                last.then_inc(vr_done, 1)

            def project_gate(n, a, c):
                if c == 0:
                    pe.wait_ge(vr_evac, n + 1)
                else:
                    pe.wait_ge(g_evac, 2 * n + 1)
                cols = xs[a][:, CH * c:CH * c + CH]
                mm(ps_m[:, 0:CH], lhsT=w_hi[:, G0:G0 + P], rhs=cols, start=True, stop=False)
                mm(ps_m[:, 0:CH], lhsT=w_lo[:, G0:G0 + P], rhs=cols, start=False, stop=True).then_inc(g_done, 1)

            def turn2(g, a, att):
                if att:
                    pe.wait_ge(g_evac, 2 * (g + 2) + 2)
                need(pe, yall_done, g)
                need(pe, x1_done, g + 1)
                turn(g, a, lo2_ready, t2_done)

            def router(g):
                pe.wait_ge(xs2_done, g + 1)
                for t in range(T):
                    mm(ps_m[:, E * t:E * t + E], lhsT=xs2[:, t, :], rhs=w_hi[:, R0:R0 + E], start=True, stop=False)
                    last = mm(ps_m[:, E * t:E * t + E], lhsT=xs2[:, t, :], rhs=w_lo[:, R0:R0 + E], start=False, stop=True)
                last.then_inc(rt_done, 1)

            def project_out(g, att, ex):
                if att:
                    pe.wait_ge(g_evac, 2 * (g + 1) + 2)
                if ex:
                    pe.wait_ge(lg_done, g)
                pe.wait_ge(ogl_done, 4 * g + 4)
                for t in range(T):
                    o = ps_m[:, D * t:D * t + D]
                    mm(o, lhsT=og_hi[:, t:TG:T], rhs=w_hi[:, O0:O0 + D], start=True, stop=False)
                    mm(o, lhsT=og_hi[:, t:TG:T], rhs=w_lo[:, O0:O0 + D], start=False, stop=False)
                    last = mm(o, lhsT=og_lo[:, t:TG:T], rhs=w_hi[:, O0:O0 + D], start=False, stop=True)
                last.then_inc(wo_done, 1)

            def experts(g, t, wo):
                if t == 0:
                    pe.wait_ge(lg_done, g + 1)
                    if wo: pe.wait_ge(x1_done, g + 2)
                elif t == 2:
                    pe.wait_ge(ct_evac, g + 1)
                else:
                    pe.wait_ge(prod_done, 5 * g + t)
                mm(ps_m[:], lhsT=xs2[:, t, :], rhs=w_hi[:, X0:X0 + 512], start=True, stop=False)
                mm(ps_m[:], lhsT=xs2[:, t, :], rhs=w_lo[:, X0:X0 + 512], start=False, stop=True).then_inc(e_done, 1)

            def turn_coef(g):
                pe.wait_ge(prod_done, 5 * g + 2)
                pe.wait_ge(rt_step, 21 * g + 21)
                pe.transpose(ps_m16[:, 0:P], c_stack[:], ident16[:]).then_inc(ct_done, 1)

            def expert_bias(g):
                pe.wait_ge(prod_done, 5 * g + 5)
                for t in range(T):
                    last = mm(ps_m[:, D * t:D * t + D], lhsT=c_t[:], rhs=eb_sel[:, t, :], start=True, stop=True)
                last.then_inc(cb_done, 1)

            def step(n, a, do):
                att, wo, ex, more = do
                b = 1 - a
                if att: scores(n, 0, 0, a)
                if att: project_v(n, a)
                if att: scores(n, 0, 1, a)
                if att: project_v_rest(n, a)
                if wo: alpha(n - 1, 3)
                if att: y_of(n, 1, 0, a)
                if wo: beta(n - 1, 3)
                if att: project_gate(n, a, 0)
                if wo: attend(n - 1, 2, b)
                if att: y_of(n, 1, 1, a)
                if att: project_gate(n, a, 1)
                if att: scores(n, 1, 0, a)
                if ex: turn2(n - 2, a, att)
                if att: scores(n, 1, 1, a)
                if att: alpha(n, 0)
                if att: y_of(n, 1, 2, a)
                if att: beta(n, 0)
                if ex: router(n - 2)
                more_beta[0] = bool(att)
                if wo: attend(n - 1, 3, b)
                more_beta[0] = True
                if att: y_of(n, 1, 3, a)
                if att: scores(n, 2, 0, a)
                if att: scores(n, 2, 1, a)
                if wo: project_out(n - 1, att, ex)
                if att: alpha(n, 1)
                if more: y_of(n + 1, 0, 0, b)
                if att: beta(n, 1)
                if ex: experts(n - 2, 0, wo)
                if att: attend(n, 0, a)
                if more: y_of(n + 1, 0, 1, b)
                if ex: experts(n - 2, 1, wo)
                if att: scores(n, 3, 0, a)
                if ex: turn_coef(n - 2)
                if att: scores(n, 3, 1, a)
                if ex: experts(n - 2, 2, wo)
                if att: alpha(n, 2)
                if more: y_of(n + 1, 0, 2, b)
                if att: beta(n, 2)
                if ex: experts(n - 2, 3, wo)
                if att: attend(n, 1, a)
                if more: y_of(n + 1, 0, 3, b)
                if ex: experts(n - 2, 4, wo)
                if ex: expert_bias(n - 2)

            for h in range(H):
                y_of(0, 0, h, 0)
            pe.wait_ge(b_ready, 1)
            run_steps(pe, step)


_INS = ["x", "WqT", "WkT", "Wv", "Wg", "Wo", "Wb", "router_w", "router_b", "expert_w", "expert_b", "mask"]


def kernel(x, L0_conv_mask, L0_conv_Wq, L0_conv_Wk, L0_conv_Wv, L0_conv_Wg, L0_conv_Wo, L0_conv_Wb,
           L0_ffn_router_w, L0_ffn_router_b, L0_ffn_expert_w, L0_ffn_expert_b):
    import numpy as np
    import concourse.bacc as bacc
    from concourse.bass_utils import run_bass_kernel_spmd

    turned = lambda w: np.concatenate([np.asarray(w).T, np.asarray(w).T], axis=1)
    given = {"x": x, "WqT": turned(L0_conv_Wq), "WkT": turned(L0_conv_Wk), "Wv": L0_conv_Wv, "Wg": L0_conv_Wg,
             "Wo": L0_conv_Wo, "Wb": L0_conv_Wb, "router_w": L0_ffn_router_w, "router_b": L0_ffn_router_b,
             "expert_w": L0_ffn_expert_w, "expert_b": L0_ffn_expert_b, "mask": np.asarray(L0_conv_mask).view(np.uint8)}
    nc = bacc.Bacc("TRN2", target_bir_lowering=False, num_devices=1)
    arrays, args = {}, []
    for name in _INS:
        a = np.ascontiguousarray(given[name])
        arrays[f"in_{name}"] = a
        args.append(nc.dram_tensor(f"in_{name}", a.shape, mybir.dt.from_np(a.dtype), kind="ExternalInput").ap())
    out = nc.dram_tensor("out_0", np.asarray(x).shape, F32, kind="ExternalOutput").ap()
    build(nc, *args, out)
    r = run_bass_kernel_spmd(nc, [arrays], core_ids=[0])
    return r.results[0]["out_0"]
```

```python
from contextlib import ExitStack

import concourse.bass as bass
from concourse import mybir

ALU = mybir.AluOpType
ACT = mybir.ActivationFunctionType
AX = mybir.AxisListType
F32 = mybir.dt.float32
F16 = mybir.dt.float16

P = 128
N = 160
D = 64
H = 4
DH = 32
E = 8
RG = 4
TG = RG * N
T = TG // P
GROUPS = N // RG
PAIRS = GROUPS // 2
T2 = 2 * T
REST = N - P
CH = TG // 2
NT = H + 1
UP = 16.0
SCALE = DH ** -0.5
EPS1, EPS2 = 1e-6, 1e-5
FAR = 1e30
ROOT_D = float(D) ** 0.5


def need(eng, sem, value):
    if isinstance(value, int) and value <= 0:
        return
    eng.wait_ge(sem, value)


def build(nc, x, WqT, WkT, Wv, Wg, Wo, Wb, router_w, router_b, expert_w, expert_b, mask, out):
    with ExitStack() as ctx:
        def sb(name, shape, dt=F32):
            return ctx.enter_context(nc.sbuf_tensor(name, shape, dt))

        def sem(name):
            return ctx.enter_context(nc.semaphore(name))

        ps_scores = [[ctx.enter_context(nc.psum_tensor(f"ps_scores{a}{b}", [P, 512], F32))
                      for b in range(2)] for a in range(2)]
        ps_y = ctx.enter_context(nc.psum_tensor("ps_y", [P, 512], F32))
        ps_pt = ctx.enter_context(nc.psum_tensor("ps_pt", [P, 512], F32))
        ps_o = ctx.enter_context(nc.psum_tensor("ps_o", [P, 512], F32))
        ps_m = ctx.enter_context(nc.psum_tensor("ps_m", [P, 512], F32))
        ps_m16 = ps_m[:].bitcast(F16)
        turned16 = [[ps_m16, ps_pt[:].bitcast(F16)], [ps_scores[0][k][:].bitcast(F16) for k in range(2)]]
        ps_bias = [ps_y, ps_o]

        ident = sb("ident", [P, P])
        ident16 = sb("ident16", [P, P], F16)
        headmask = sb("headmask", [P, H])
        half = sb("half", [P, T2])
        eps1, eps2 = sb("eps1", [P, T2]), sb("eps2", [P, T2])
        order = sb("order", [P, T, E])
        w_raw = sb("w_raw", [P, 844])
        w_hi = sb("w_hi", [P, 844], F16)
        w_lo = sb("w_lo", [P, 844], F16)
        qk_raw = sb("qk_raw", [P, 2, P])
        g_hi = sb("g_hi", [P, H, P], F16)
        g_lo = sb("g_lo", [P, H, P], F16)
        rb = sb("rb", [P, T, E])
        eb_raw = sb("eb_raw", [P, T, D])
        eb_hi = sb("eb_hi", [P, T, D], F16)
        eb_diff = sb("eb_diff", [P, T, D])
        eb_sel = sb("eb_sel", [P, T, D], F16)
        is_lo = sb("is_lo", [P, 2])
        bias32 = sb("bias32", [P, NT, N])
        bias_hi = sb("bias_hi", [P, NT, N], F16)
        bias_lo = sb("bias_lo", [P, NT, N], F16)
        V0, G0, X0, R0, B0, O0 = 0, 128, 256, 768, 776, 780

        xin = [sb(f"xin{a}", [P, T2, D]) for a in range(2)]
        ln_s = [sb(f"ln_s{a}", [P, 4, T2]) for a in range(2)]
        xc = [sb(f"xc{a}", [P, T2, D]) for a in range(2)]
        sq = [sb(f"sq{a}", [P, T2, D]) for a in range(2)]
        xn = [sb(f"xn{a}", [P, T2, D]) for a in range(2)]
        hl = [sb(f"hl{a}", [P, T2, 2, D], F16) for a in range(2)]
        ln_v = [sb(f"ln_v{a}", [P, T2]) for a in range(2)]
        xs_pair = [sb(f"xs_pair{a}", [P, 2 * TG], F16) for a in range(2)]
        xs_all = sb("xs_all", [P, GROUPS * TG], F16)
        wb = sb("wb", [P, 2, 32], F16)
        mask_u8 = sb("mask_u8", [P, N], mybir.dt.uint8)
        pen = sb("pen", [P, N])
        xs_mask = [sb(f"xs_mask{a}", [P, TG], F16) for a in range(2)]
        b_stage = [sb(f"b_stage{a}", [P, 2, N]) for a in range(2)]
        xs = [sb(f"xs{a}", [P, TG], F16) for a in range(2)]
        y_hi = [sb(f"y_hi{c}", [P, H, CH], F16) for c in range(2)]
        y_lo = [sb(f"y_lo{c}", [P, H, CH], F16) for c in range(2)]
        v_main = [sb(f"v_main{a}", [P, RG, P]) for a in range(2)]
        v_bd = [sb(f"v_bd{a}", [P, RG, H, DH]) for a in range(2)]
        gate = [sb(f"gate{a}", [P, TG]) for a in range(2)]
        negmax = [sb(f"negmax{a}", [P, NT]) for a in range(2)]
        psum_row = [sb(f"psum_row{a}", [P, NT]) for a in range(2)]
        rinv = [sb(f"rinv{a}", [P, NT]) for a in range(2)]
        probs = [sb(f"probs{a}", [P, NT, N]) for a in range(2)]
        pn_main = [sb(f"pn_main{a}", [P, H, P]) for a in range(2)]
        pn_rest = [sb(f"pn_rest{a}", [P, H, REST]) for a in range(2)]
        pn_pack = [sb(f"pn_pack{a}", [P, N]) for a in range(2)]
        pt_main = [sb(f"pt_main{a}", [P, H, N]) for a in range(2)]
        pt_pack = [sb(f"pt_pack{a}", [P, N]) for a in range(2)]
        og = sb("og", [P, TG])
        og_hi = sb("og_hi", [P, TG], F16)
        og_lo = sb("og_lo", [P, TG], F16)
        x1 = [sb(f"x1_{a}", [P, T, D]) for a in range(2)]
        xs2 = sb("xs2", [P, T, P], F16)
        lg = sb("lg", [P, T, E])
        rt = sb("rt", [P, 8, T, E])
        rs = sb("rs", [P, 12, T])
        coef = sb("coef", [P, T, E])
        c_stack = sb("c_stack", [P, P], F16)
        c_t = sb("c_t", [P, P], F16)
        prod = [sb(f"prod{a}", [P, 8, D]) for a in range(2)]
        add1 = [sb(f"add1{a}", [P, 4, D]) for a in range(2)]
        add2 = [sb(f"add2{a}", [P, 2, D]) for a in range(2)]
        ymix = sb("ymix", [P, T, D])
        yall = sb("yall", [P, T, D])
        res = [sb(f"res{a}", [P, T, D]) for a in range(2)]

        b_dram = nc.dram_tensor("bias_scratch", [N, 32, N], F32, kind="Internal").ap()

        wb_loaded, w_loaded, const_ready = sem("wb_loaded"), sem("w_loaded"), sem("const_ready")
        wprep, wb_ready, gprod_done, w_ready = sem("wprep"), sem("wb_ready"), sem("gprod_done"), sem("w_ready")
        x_loaded = [sem(f"x_loaded{a}") for a in range(2)]
        sq_done, sq2_done = sem("sq_done"), sem("sq2_done")
        lnA, lnP, lnS, hi_ready, lo_ready = sem("lnA"), sem("lnP"), sem("lnS"), sem("hi_ready"), sem("lo_ready")
        t1_done, xs_made, b_done, b_evac = sem("t1_done"), sem("xs_made"), sem("b_done"), sem("b_evac")
        xs_kept = [sem(f"xs_kept{a}") for a in range(2)]
        b_written = [sem(f"b_written{a}") for a in range(2)]
        b_loaded, b_ready = [sem(f"b_loaded{k}") for k in range(2)], sem("b_ready")
        xs_loaded = [sem(f"xs_loaded{a}") for a in range(2)]
        y_done, yhi_done, ylo_done = sem("y_done"), sem("yhi_done"), sem("ylo_done")
        s_done, max_done, exp_done = sem("s_done"), sem("max_done"), sem("exp_done")
        rinv_done, pnm_done, pnr_done, tr_done = sem("rinv_done"), sem("pnm_done"), sem("pnr_done"), sem("tr_done")
        alpha_done, beta_done, ptm_done, ptb_done = sem("alpha_done"), sem("beta_done"), sem("ptm_done"), sem("ptb_done")
        v_done, v_evac, vr_done, vr_evac = sem("v_done"), sem("v_evac"), sem("vr_done"), sem("vr_evac")
        g_done, g_evac = sem("g_done"), sem("g_evac")
        av_done, og_done, ogh_done, ogl_done = sem("av_done"), sem("og_done"), sem("ogh_done"), sem("ogl_done")
        wo_done, x1_done = sem("wo_done"), sem("x1_done")
        ln2A, ln2P, ln2S, hi2_ready, lo2_ready = sem("ln2A"), sem("ln2P"), sem("ln2S"), sem("hi2_ready"), sem("lo2_ready")
        t2_done, xs2_done = sem("t2_done"), sem("xs2_done")
        rt_done, lg_done, rt_step, rt_exp = sem("rt_done"), sem("lg_done"), sem("rt_step"), sem("rt_exp")
        c_ready, ct_done, ct_evac = sem("c_ready"), sem("ct_done"), sem("ct_evac")
        e_done, prod_done, mix_step, cb_done, yall_done, res_done = (
            sem("e_done"), sem("prod_done"), sem("mix_step"), sem("cb_done"), sem("yall_done"), sem("res_done"))
        res_stored = [sem(f"res_stored{a}") for a in range(2)]

        x_flat = x.rearrange("a r j d -> (a r j d)")
        out_flat = out.rearrange("a r j d -> (a r j d)")
        b_flat = b_dram.rearrange("r h j -> (r h j)")
        tokens = lambda flat, start: flat[bass.ds(start, TG * D)].rearrange("(p t d) -> p t d", p=P, t=T)
        KE = ctx.enter_context(nc.Block())

        def pairs_loop(eng, body, first, end):
            with eng.Fori(0, (end - first) // 2) as i:
                body(i * 2 + first, first % 2)
                body(i * 2 + (first + 1), 1 - first % 2)

        N_CONST = 16 + 1 + 2
        def run_phase1(eng, step):
            for n in range(5):
                step(n, n % 2, (1, n >= 1, n >= 2, n >= 3))
            pairs_loop(eng, lambda n, a: step(n, a, (1, 1, 1, 1)), 5, PAIRS - 1)
            for n in range(PAIRS - 1, PAIRS + 3):
                step(n, n % 2, (n < PAIRS, n - 1 < PAIRS, n - 2 < PAIRS, n - 3 < PAIRS))

        def run_steps(eng, step):
            step(0, 0, (1, 0, 0, 0, 1))
            step(1, 1, (1, 1, 0, 0, 1))
            step(2, 0, (1, 1, 1, 0, 1))
            pairs_loop(eng, lambda n, a: step(n, a, (1, 1, 1, 1, 1)), 3, GROUPS - 1)
            step(GROUPS - 1, 1, (1, 1, 1, 1, 0))
            step(GROUPS, 0, (0, 1, 1, 1, 0))
            step(GROUPS + 1, 1, (0, 0, 1, 1, 0))
            step(GROUPS + 2, 0, (0, 0, 0, 1, 0))

        def back(n, r, k, do):
            return (n, r - k, do[0]) if r >= k else (n - 1, r - k + RG, do[1])

        N_WLOAD = 2 * 4 + 3 + T + 3 * T + 1

        @KE.sync
        def _(sp):
            def at(g, size):
                return g * size if isinstance(g, int) else sp.snap(g * size)

            def load_x(m, a):
                start = at(m, 2 * TG * D)
                need(sp, lnA, 3 * m - 3)
                sp.dma_start(xin[a][:], x_flat[bass.ds(start, 2 * TG * D)].rearrange("(p t d) -> p t d", p=P, t=T2)).then_inc(x_loaded[a], 16)

            def keep_xs(m, a):
                start = at(m, 2 * TG)
                sp.wait_ge(xs_made, m + 1)
                sp.dma_start(xs_all[:, bass.ds(start, 2 * TG)], xs_pair[a][:]).then_inc(xs_kept[a], 16)

            def store_bias(m, a):
                start = at(m, 2 * P * N)
                sp.wait_ge(b_evac, m + 1)
                sp.dma_start(b_flat[bass.ds(start, 2 * P * N)].rearrange("(k p j) -> p k j", k=2, p=P), b_stage[a][:]).then_inc(b_written[a], 16)

            for m in range(2):
                load_x(m, m)
            for half_ in range(2):
                sp.dma_start(w_raw[64 * half_:64 * half_ + 64, B0:B0 + 4], Wb).then_inc(wb_loaded, 16)
            ld = lambda dst, src: sp.dma_start(dst, src).then_inc(w_loaded, 16)
            for half_ in range(2):
                rows = slice(64 * half_, 64 * half_ + 64)
                ld(w_raw[rows, V0:V0 + 128], Wv)
                ld(w_raw[rows, G0:G0 + 128], Wg)
                ld(w_raw[rows, X0:X0 + 512].rearrange("p (e c) -> p e c", e=E), expert_w.rearrange("e d c -> d e c"))
                ld(w_raw[rows, R0:R0 + 8], router_w)
                load_x(2 + half_, half_)
            ld(w_raw[:, O0:O0 + 64], Wo)
            ld(qk_raw[:, 0, :], WqT)
            ld(qk_raw[:, 1, :], WkT)
            ld(mask_u8[D:P, :], mask.broadcast_to([P - D, N]))
            load_x(4, 0)
            keep_xs(0, 0)
            for t in range(T):
                ld(rb[:, t, :], router_b.rearrange("(a e) -> a e", a=1).broadcast_to([P, E]))
            load_x(5, 1)
            keep_xs(1, 1)
            store_bias(0, 0)
            sp.wait_ge(const_ready, 1)

            def load_eb(part):
                for t in range(T):
                    ld(eb_raw[40 * part + 8 * t:40 * part + 8 * t + 8, t, :], expert_b)

            load_eb(0)
            load_x(6, 0)
            keep_xs(2, 0)
            store_bias(1, 1)
            load_eb(1)
            load_x(7, 1)
            keep_xs(3, 1)
            store_bias(2, 0)
            load_eb(2)

            def phase1(n, a):
                load_x(n + 1, 1 - a)
                keep_xs(n - 3, 1 - a)
                store_bias(n - 4, a)

            pairs_loop(sp, phase1, 7, PAIRS - 1)
            for n in range(PAIRS - 1, PAIRS + 4):
                if n + 1 < PAIRS: load_x(n + 1, 1 - n % 2)
                if n - 3 < PAIRS: keep_xs(n - 3, 1 - n % 2)
                store_bias(n - 4, n % 2)
                if n == PAIRS + 1:
                    for a in range(2):
                        sp.wait_ge(b_written[a], 16 * (P // (2 * RG) // 2))
                    sp.dma_start(bias32[:, 0:H, :], b_dram[0:P, 0:H, :]).then_inc(b_loaded[0], 16)

            def load_xs(g, a):
                start = at(g, TG)
                need(sp, s_done, 8 * (g - 1))
                sp.dma_start(xs[a][:], xs_all[:, bass.ds(start, TG)]).then_inc(xs_loaded[a], 16)
                sp.dma_start(xs_mask[a][0:D, :], xs_all[0:D, bass.ds(start, TG)]).then_inc(xs_loaded[a], 16)

            load_xs(0, 0)
            load_xs(1, 1)
            for a in range(2):
                sp.wait_ge(b_written[a], 16 * (PAIRS // 2))
            for h in range(H):
                sp.dma_start(bias32[32 * h:32 * h + 32, H, :], b_dram[P:N, h, :]).then_inc(b_loaded[1], 16)

            def load_res(g, a):
                start = at(g, TG * D)
                need(sp, x1_done, g - 1)
                sp.dma_start(xin[a][:, 0:T], tokens(x_flat, start)).then_inc(x_loaded[a], 16)

            def store(g, a):
                start = at(g, TG * D)
                sp.wait_ge(res_done, g + 1)
                sp.dma_start(tokens(out_flat, start), res[a][:]).then_inc(res_stored[a], 16)

            for a in range(2):
                sp.wait_ge(xs_kept[a], 16 * (PAIRS // 2))
            for g in range(2):
                load_res(g, g)

            def phase2(g, a):
                load_xs(g, a)
                load_res(g, a)
                store(g - 4, a)

            for g in range(2, 4):
                load_xs(g, g % 2)
                load_res(g, g % 2)
            pairs_loop(sp, phase2, 4, GROUPS)
            for g in range(GROUPS - 4, GROUPS):
                store(g, g % 2)
            for a in range(2):
                sp.wait_ge(res_stored[a], 16 * (GROUPS // 2))

        @KE.gpsimd
        def _(pool):
            pool.memset(eb_raw[:], 0.0).then_inc(const_ready, 1)
            pool.memset(ident[:], 0.0).then_inc(const_ready, 1)
            pool.memset(headmask[:], 0.0).then_inc(const_ready, 1)
            pool.memset(half[:], -0.5).then_inc(const_ready, 1)
            pool.memset(eps1[:], D * EPS1).then_inc(const_ready, 1)
            pool.memset(eps2[:], D * EPS2).then_inc(const_ready, 1)
            pool.memset(c_stack[:], 0.0).then_inc(const_ready, 1)
            pool.memset(is_lo[:], 0.0).then_inc(const_ready, 1)
            for e in range(E):
                pool.memset(order[:, :, e], float(E - e)).then_inc(const_ready, 1)
            pool.wait_ge(const_ready, 16)
            pool.affine_select(out=ident[:], in_=ident[:], compare_op=ALU.not_equal, fill=1.0, base=0,
                               pattern=[[-1, P]], channel_multiplier=1).then_inc(const_ready, 1)
            pool.affine_select(out=is_lo[:, 0:1], in_=is_lo[:, 0:1], compare_op=ALU.is_gt, fill=1.0, base=80,
                               pattern=[[0, 1]], channel_multiplier=-1).then_inc(const_ready, 1)
            pool.affine_select(out=is_lo[:, 1:2], in_=is_lo[:, 1:2], compare_op=ALU.is_ge, fill=1.0, base=-80,
                               pattern=[[0, 1]], channel_multiplier=1).then_inc(const_ready, 1)

            def ln_scale(g, a, w, sums, step, eps, own):
                pool.wait_ge(sums, g + 1)
                pool.tensor_tensor(ln_v[a][:, 0:w], ln_s[a][:, 2, 0:w], eps[:, 0:w], ALU.add).then_inc(own, 1)
                pool.wait_ge(own, 3 * g + 1)
                pool.tensor_tensor(ln_s[a][:, 3, 0:w], ln_v[a][:, 0:w], half[:, 0:w], ALU.pow).then_inc(own, 1)
                pool.wait_ge(own, 3 * g + 2)
                need(pool, step, g - 1)
                pool.tensor_tensor(xn[a][:, 0:w], xc[a][:, 0:w], ln_s[a][:, 3, 0:w].unsqueeze(2).broadcast_to([P, w, D]),
                                   ALU.mult).then_inc(own, 1)

            def phase1(n, a, do):
                if do[1]: ln_scale(n - 1, 1 - a, T2, lnS, lo_ready, eps1, lnP)

            run_phase1(pool, phase1)

            def norm_main(g, r):
                a = r % 2
                pool.wait_ge(rinv_done, 4 * g + r + 1)
                need(pool, beta_done, 4 * g + r - 1)
                pool.tensor_tensor(pn_main[a][:], probs[a][:, 0:H, 0:P],
                                   rinv[a][:, 0:H].unsqueeze(2).broadcast_to([P, H, P]), ALU.mult).then_inc(pnm_done, 1)

            def og_low(g, r):
                pool.wait_ge(ogh_done, 4 * g + r + 1)
                pool.tensor_tensor(og_lo[:, N * r:N * r + N], og[:, N * r:N * r + N], og_hi[:, N * r:N * r + N],
                                   ALU.subtract).then_inc(ogl_done, 1)

            def mix(g, t):
                a, b = t % 2, 15 * g + 3 * t
                pool.wait_ge(prod_done, 5 * g + t + 1)
                pool.tensor_tensor(add1[a][:], prod[a][:, 0:4, :], prod[a][:, 4:8, :], ALU.add).then_inc(mix_step, 1)
                pool.wait_ge(mix_step, b + 1)
                pool.tensor_tensor(add2[a][:], add1[a][:, 0:2, :], add1[a][:, 2:4, :], ALU.add).then_inc(mix_step, 1)
                pool.wait_ge(mix_step, b + 2)
                if t == 0:
                    need(pool, yall_done, g)
                pool.tensor_tensor(ymix[:, t, :], add2[a][:, 0, :], add2[a][:, 1, :], ALU.add).then_inc(mix_step, 1)

            def step(n, a, do):
                att, wo, ex, fin, _ = do
                for r in range(RG):
                    if wo: og_low(n - 1, r)
                    if r == 2 and fin: mix(n - 3, 2)
                    g1, r1, on = back(n, r, 1, do)
                    if on: norm_main(g1, r1)
                    if r == 0 and ex: ln_scale(n - 2, a, T, ln2S, lo2_ready, eps2, ln2P)
                    if r == 1 and fin: mix(n - 3, 0)
                    if r == 1 and fin: mix(n - 3, 1)
                    if r == 2 and fin: mix(n - 3, 3)
                    if r == 3 and fin: mix(n - 3, 4)

            run_steps(pool, step)


        @KE.scalar
        def _(act):
            def square(g, a, w, src_done, sums, own):
                act.wait_ge(src_done, 3 * g + 3)
                need(act, sums, g - 1)
                act.activation(sq[a][:, 0:w], xc[a][:, 0:w], ACT.Square).then_inc(own, 1)

            def high(g, a, w, scaled, transposed, own):
                act.wait_ge(scaled, 3 * g + 3)
                need(act, transposed, g - 1)
                act.activation(hl[a][:, 0:w, 0, :], xn[a][:, 0:w], ACT.Copy, scale=ROOT_D).then_inc(own, 1)

            def make_xs(m, a):
                act.wait_ge(t1_done, m + 1)
                need(act, b_done, m - 1)
                need(act, xs_kept[a], 8 * m - 8 * a)
                for k in range(2):
                    i = act.activation(xs_pair[a][:].rearrange("c (p t) -> c t p", t=T2)[:, T * k:T * k + T],
                                       turned16[a][k][:, 0:TG].rearrange("c (t p) -> c t p", t=T), ACT.Copy)
                i.then_inc(xs_made, 1)

            def phase1(n, a, do):
                if do[0]: square(n, a, T2, lnA, lnS, sq_done)
                if do[2]: make_xs(n - 2, a)
                if do[1]: high(n - 1, 1 - a, T2, lnP, t1_done, hi_ready)

            run_phase1(act, phase1)

            def exp(n, r, u):
                a, k0, k1 = r % 2, (0, 3)[u], (3, NT)[u]
                act.wait_ge(max_done, 8 * n + 2 * r + u + 1)
                need(act, pnm_done, 4 * n + r - 1)
                need(act, pnr_done, 2 * (4 * n + r - 1))
                for k in range(k0, k1):
                    e = act.activation(probs[a][:, k, :], ps_scores[a][u][:, (k - k0) * N:(k - k0 + 1) * N], ACT.Exp,
                                       bias=negmax[a][:, k:k + 1], accum_out=psum_row[a][:, k:k + 1])
                e.then_inc(exp_done, 1)

            def pt_alpha(n, r):
                q, a = 4 * n + r, r % 2
                act.wait_ge(alpha_done, q + 1)
                need(act, av_done, q - 1)
                act.activation(pt_main[a][:, :, 0:P], ps_pt[:].rearrange("j (h i) -> j h i", h=H),
                               ACT.Copy).then_inc(ptm_done, 1)

            def pt_beta(n, r):
                q, a = 4 * n + r, r % 2
                act.wait_ge(beta_done, q + 1)
                act.activation(pt_main[a][:, :, P:N], ps_o[:, N:N + P].rearrange("j (h i) -> j h i", h=H),
                               ACT.Copy).then_inc(ptb_done, 1)
                act.activation(pt_pack[a][:, 0:P], ps_o[:, N + P:N + 2 * P], ACT.Copy).then_inc(ptb_done, 1)

            def y_high(g, c, h):
                act.wait_ge(y_done, 8 * g + 4 * c + h + 1)
                need(act, s_done, 8 * (g - 1) + 4 * (c + 1))
                act.activation(y_hi[c][:, h, :], ps_y[:, 0:CH], ACT.Copy, scale=1.0 / UP).then_inc(yhi_done, 1)

            def og_high(n, r):
                act.wait_ge(og_done, 4 * n + r + 1)
                need(act, wo_done, n)
                act.activation(og_hi[:, N * r:N * r + N], og[:, N * r:N * r + N], ACT.Copy).then_inc(ogh_done, 1)

            def keep_v(n, a):
                act.wait_ge(v_done, n + 1)
                need(act, av_done, 4 * (n - 1))
                act.activation(v_main[a][:], ps_m[:].rearrange("j (r e) -> j r e", r=RG), ACT.Copy,
                               scale=1.0 / UP).then_inc(v_evac, 1)

            def tanh_gate(n, a, c):
                act.wait_ge(g_done, 2 * n + c + 1)
                need(act, og_done, 4 * (n - 1))
                act.activation(gate[a][:, CH * c:CH * c + CH], ps_m[:, 0:CH], ACT.Tanh,
                               scale=0.5 / UP).then_inc(g_evac, 1)

            def keep_xs2(g):
                act.wait_ge(t2_done, g + 1)
                need(act, e_done, 5 * g)
                act.activation(xs2[:], ps_m16[:, 0:TG].rearrange("c (t p) -> c t p", t=T), ACT.Copy).then_inc(xs2_done, 1)

            def router_exp(g):
                act.wait_ge(rt_step, 21 * g + 12)
                act.activation(rs[:, 5, :], rs[:, 4, :], ACT.Exp, scale=1.0 / UP).then_inc(rt_exp, 1)

            def keep_coef(g):
                act.wait_ge(ct_done, g + 1)
                act.activation(c_t[:], ps_m16[:, 0:P], ACT.Copy).then_inc(ct_evac, 1)

            def step(n, a, do):
                att, wo, ex, fin, more = do
                for r in range(RG):
                    g1, r1, on1 = back(n, r, 1, do)
                    g2, r2, on2 = back(n, r, 2, do)
                    g3, r3, on3 = back(n, r, 3, do)
                    if on1: exp(g1, r1, 1)
                    if r == 0 and att: keep_v(n, a)
                    if r == 0 and ex: square(n - 2, a, T, ln2A, ln2S, sq2_done)
                    if r == 0 and att: y_high(n, 1, 0)
                    if r == 1 and att: y_high(n, 1, 3)
                    if r == 2 and more: y_high(n + 1, 0, 1)
                    if att: exp(n, r, 0)
                    if r == 2 and ex: keep_xs2(n - 2)
                    if on2: pt_alpha(g2, r2)
                    if r == 0 and att: y_high(n, 1, 1)
                    if r == 2 and more: y_high(n + 1, 0, 2)
                    if on2: pt_beta(g2, r2)
                    if r == 2 and fin: keep_coef(n - 3)
                    if r == 0 and att: tanh_gate(n, a, 0)
                    if r == 1 and ex: high(n - 2, a, T, ln2P, t2_done, hi2_ready)
                    if r == 0 and att: y_high(n, 1, 2)
                    if r == 1 and more: y_high(n + 1, 0, 0)
                    if r == 2 and more: y_high(n + 1, 0, 3)
                    if on3: og_high(g3, r3)
                    if r == 0 and att: tanh_gate(n, a, 1)
                    if r == 3 and ex: router_exp(n - 2)

            for h in range(H):
                y_high(0, 0, h)
            run_steps(act, step)

        @KE.vector
        def _(dve):
            made = [0]

            def prep(ins):
                ins.then_inc(wprep, 1)
                made[0] += 1
                dve.wait_ge(wprep, made[0])

            for c in range(2):
                prep(dve.memset(y_lo[c][D:P, :, :], 32768.0))
            prep(dve.memset(wb[:], 0.0))
            dve.wait_ge(const_ready, N_CONST)
            for h in range(H):
                prep(dve.memset(headmask[32 * h:32 * h + 32, h:h + 1], 1.0 / UP))
            prep(dve.tensor_copy(ident16[:], ident[:]))
            dve.wait_ge(wb_loaded, 32)
            prep(dve.tensor_scalar(wb[:, 0, 0:H], w_raw[:, B0:B0 + H], UP, None, ALU.mult))
            prep(dve.scalar_tensor_tensor(out=wb[:, 1, 0:H], in0=w_raw[:, B0:B0 + H], scalar=UP, in1=wb[:, 0, 0:H],
                                          op0=ALU.mult, op1=ALU.subtract))
            dve.nop().then_inc(wb_ready, 1)

            def total(g, a, w, src, own):
                dve.tensor_reduce(ln_s[a][:, 0, 0:w], src[a][:, 0:w], AX.X, ALU.add).then_inc(own, 1)

            def mean(g, a, w, own):
                dve.wait_ge(own, 3 * g + 1)
                dve.tensor_scalar(ln_s[a][:, 1, 0:w], ln_s[a][:, 0, 0:w], -1.0 / D, None, ALU.mult).then_inc(own, 1)

            def center(g, a, w, src, own, used_by_square, used_by_scale):
                dve.wait_ge(own, 3 * g + 2)
                need(dve, used_by_square, g - 1)
                need(dve, used_by_scale, 3 * (g - 1))
                dve.tensor_tensor(xc[a][:, 0:w], src[a][:, 0:w], ln_s[a][:, 1, 0:w].unsqueeze(2).broadcast_to([P, w, D]),
                                  ALU.add).then_inc(own, 1)

            def sum_squares(g, a, w, squared, scaled, own):
                dve.wait_ge(squared, g + 1)
                need(dve, scaled, 3 * (g - 1))
                dve.tensor_reduce(ln_s[a][:, 2, 0:w], sq[a][:, 0:w], AX.X, ALU.add).then_inc(own, 1)

            def low(g, a, w, high_done, own):
                dve.wait_ge(high_done, g + 1)
                dve.scalar_tensor_tensor(out=hl[a][:, 0:w, 1, :], in0=xn[a][:, 0:w], scalar=ROOT_D, in1=hl[a][:, 0:w, 0, :],
                                         op0=ALU.mult, op1=ALU.subtract).then_inc(own, 1)

            def weight_halves():
                dve.wait_ge(w_loaded, 16 * N_WLOAD)
                prep(dve.tensor_scalar(w_hi[:, 0:B0], w_raw[:, 0:B0], UP, None, ALU.mult))
                prep(dve.tensor_scalar(w_hi[:, O0:O0 + D], w_raw[:, O0:O0 + D], UP, None, ALU.mult))
                prep(dve.scalar_tensor_tensor(out=w_lo[:, 0:B0], in0=w_raw[:, 0:B0], scalar=UP, in1=w_hi[:, 0:B0],
                                              op0=ALU.mult, op1=ALU.subtract))
                prep(dve.scalar_tensor_tensor(out=w_lo[:, O0:O0 + D], in0=w_raw[:, O0:O0 + D], scalar=UP, in1=w_hi[:, O0:O0 + D],
                                              op0=ALU.mult, op1=ALU.subtract))

            def y_weights():
                dve.wait_ge(gprod_done, H)
                g_of = ps_scores[1][0][:].rearrange("p (h c) -> p h c", h=H)
                prep(dve.tensor_scalar(g_hi[:], g_of, SCALE * UP, None, ALU.mult))
                prep(dve.scalar_tensor_tensor(out=g_lo[:], in0=g_of, scalar=SCALE * UP, in1=g_hi[:], op0=ALU.mult, op1=ALU.subtract))
                prep(dve.tensor_scalar(pen[D:P, :], mask_u8[D:P, :], -1.0, 65504.0, ALU.add, ALU.mult))
                for a in range(2):
                    prep(dve.tensor_copy(xs_mask[a][D:P, :].rearrange("p (r j) -> p r j", r=RG),
                                         pen[D:P, :].unsqueeze(1).broadcast_to([P - D, RG, N])))
                dve.nop().then_inc(w_ready, 1)

            def expert_bias_halves():
                prep(dve.tensor_scalar(rb[:], rb[:], UP, None, ALU.mult))
                prep(dve.tensor_scalar(eb_hi[:], eb_raw[:], UP, None, ALU.mult))
                prep(dve.scalar_tensor_tensor(out=eb_diff[:], in0=eb_raw[:], scalar=UP, in1=eb_hi[:], op0=ALU.mult, op1=ALU.subtract))
                prep(dve.tensor_scalar(eb_diff[:], eb_diff[:], is_lo[:, 0:1], None, ALU.mult))
                prep(dve.scalar_tensor_tensor(out=eb_sel[:], in0=eb_hi[:], scalar=is_lo[:, 1:2], in1=eb_diff[:],
                                              op0=ALU.mult, op1=ALU.add))

            def phase1(n, a, do):
                if do[0]:
                    dve.wait_ge(x_loaded[a], 8 * n + 16 - 8 * a)
                    total(n, a, T2, xin, lnA)
                if do[1]: sum_squares(n - 1, 1 - a, T2, sq_done, lnP, lnS)
                if do[0]: mean(n, a, T2, lnA)
                if do[2]: low(n - 2, a, T2, hi_ready, lo_ready)
                if do[0]: center(n, a, T2, xin, lnA, sq_done, lnP)
                if do[3]:
                    dve.wait_ge(b_done, n - 2)
                    need(dve, b_written[1 - a], 8 * (n - 3) - 8 * (1 - a))
                    dve.tensor_scalar(b_stage[1 - a][:], ps_bias[1 - a][:, 0:2 * N].rearrange("p (k j) -> p k j", k=2),
                                      1.0 / UP, None, ALU.mult).then_inc(b_evac, 1)
                if not do[0]:
                    (weight_halves, y_weights, expert_bias_halves)[n - PAIRS]()

            run_phase1(dve, phase1)

            for k, part in enumerate((slice(0, H), slice(H, NT))):
                dve.wait_ge(b_loaded[k], (16, 16 * H)[k])
                prep(dve.tensor_copy(bias_hi[:, part], bias32[:, part]))
                prep(dve.tensor_tensor(bias_lo[:, part], bias32[:, part], bias_hi[:, part], ALU.subtract))
            dve.nop().then_inc(b_ready, 1)

            def row_max(n, r, u):
                a, k0, k1 = r % 2, (0, 3)[u], (3, NT)[u]
                i = 8 * n + 2 * r + u
                dve.wait_ge(s_done, i + 1)
                dve.tensor_reduce(negmax[a][:, k0:k1],
                                  ps_scores[a][u][:, 0:(k1 - k0) * N].rearrange("i (k j) -> i k j", j=N),
                                  AX.X, ALU.max, negate=True).then_inc(max_done, 1)

            def norm_rest(n, r):
                q, a = 4 * n + r, r % 2
                dve.wait_ge(exp_done, 2 * q + 2)
                need(dve, pnm_done, q - 1)
                dve.reciprocal(rinv[a][:], psum_row[a][:]).then_inc(rinv_done, 1)
                dve.wait_ge(rinv_done, q + 1)
                need(dve, beta_done, q - 1)
                need(dve, tr_done, q - 1)
                dve.tensor_scalar(pn_pack[a][:], probs[a][:, H, :], rinv[a][:, H:NT], None, ALU.mult).then_inc(pnr_done, 1)
                dve.tensor_tensor(pn_rest[a][:], probs[a][:, 0:H, P:N],
                                  rinv[a][:, 0:H].unsqueeze(2).broadcast_to([P, H, REST]), ALU.mult).then_inc(pnr_done, 1)

            def turn_rest(n, r):
                q, a = 4 * n + r, r % 2
                dve.wait_ge(pnr_done, 2 * q + 1)
                need(dve, av_done, q - 1)
                dve.transpose(pt_pack[a][:, P:N], pn_pack[a][:, P:N]).then_inc(tr_done, 1)

            def y_low(g, c, h):
                i = 8 * g + 4 * c + h
                dve.wait_ge(yhi_done, i + 1)
                dve.scalar_tensor_tensor(out=y_lo[c][0:D, h, :], in0=ps_y[0:D, 0:CH], scalar=1.0 / UP,
                                         in1=y_hi[c][0:D, h, :], op0=ALU.mult, op1=ALU.subtract).then_inc(ylo_done, 1)

            def gated(n, r, a):
                q = 4 * n + r
                dve.wait_ge(av_done, q + 1)
                dve.wait_ge(g_evac, 2 * n + 2)
                need(dve, ogl_done, q - 3)
                dve.scalar_tensor_tensor(out=og[:, N * r:N * r + N], in0=gate[a][:, N * r:N * r + N], scalar=1.0,
                                         in1=ps_o[:, 0:N], op0=ALU.add, op1=ALU.mult).then_inc(og_done, 1)

            def keep_v_rest(n, a):
                dve.wait_ge(vr_done, n + 1)
                need(dve, av_done, 4 * (n - 1))
                dve.tensor_tensor(v_bd[a][:],
                                  ps_m[:, 0:RG * DH].rearrange("j (r e) -> j r e", r=RG).unsqueeze(2).broadcast_to([P, RG, H, DH]),
                                  headmask[:].unsqueeze(1).unsqueeze(3).broadcast_to([P, RG, H, DH]),
                                  ALU.mult).then_inc(vr_evac, 1)

            def attention_out(g, a):
                dve.wait_ge(wo_done, g + 1)
                dve.wait_ge(x_loaded[a], 4 * GROUPS + 8 * g + 16 - 8 * a)
                need(dve, res_done, g - 1)
                dve.scalar_tensor_tensor(out=x1[a][:], in0=ps_m[:, 0:T * D].rearrange("p (t d) -> p t d", t=T),
                                         scalar=0.5 / UP, in1=xin[a][:, 0:T], op0=ALU.mult, op1=ALU.add).then_inc(x1_done, 1)
                dve.wait_ge(x1_done, g + 1)
                total(g, a, T, x1, ln2A)
                mean(g, a, T, ln2A)
                center(g, a, T, x1, ln2A, sq2_done, ln2P)

            wide = lambda v: v.unsqueeze(2).broadcast_to([P, T, E])

            def route(g, steps):
                L, tt, red = lg[:], dve.tensor_tensor, dve.tensor_reduce
                flat = coef[:].rearrange("p t e -> p (t e)")
                for k in steps:
                    if k == 0:
                        dve.wait_ge(rt_done, g + 1)
                        tt(L, ps_m[:, 0:T * E].rearrange("p (t e) -> p t e", t=T), rb[:], ALU.add).then_inc(lg_done, 1)
                        continue
                    if k == 1:
                        dve.wait_ge(lg_done, g + 1)
                    else:
                        dve.wait_ge(rt_step, 21 * g + k - 1)
                    if k == 13:
                        dve.wait_ge(rt_exp, g + 1)
                    if k == 1: i = red(rs[:, 0, :], L, AX.X, ALU.max)
                    if k == 2: i = tt(rt[:, 0], L, wide(rs[:, 0, :]), ALU.is_equal)
                    if k == 3: i = tt(rt[:, 1], rt[:, 0], order[:], ALU.mult)
                    if k == 4: i = red(rs[:, 1, :], rt[:, 1], AX.X, ALU.max)
                    if k == 5: i = tt(rt[:, 2], rt[:, 1], wide(rs[:, 1, :]), ALU.is_equal)
                    if k == 6: i = dve.scalar_tensor_tensor(out=rt[:, 3], in0=rt[:, 2], scalar=-FAR, in1=L,
                                                            op0=ALU.mult, op1=ALU.add)
                    if k == 7: i = red(rs[:, 2, :], rt[:, 3], AX.X, ALU.max)
                    if k == 8: i = tt(rt[:, 4], rt[:, 3], wide(rs[:, 2, :]), ALU.is_equal)
                    if k == 9: i = tt(rt[:, 5], rt[:, 4], order[:], ALU.mult)
                    if k == 10: i = red(rs[:, 3, :], rt[:, 5], AX.X, ALU.max)
                    if k == 11: i = tt(rt[:, 6], rt[:, 5], wide(rs[:, 3, :]), ALU.is_equal)
                    if k == 12: i = tt(rs[:, 4, :], rs[:, 2, :], rs[:, 0, :], ALU.subtract)
                    if k == 13: i = dve.tensor_scalar(rs[:, 6, :], rs[:, 5, :], 1.0, None, ALU.add)
                    if k == 14: i = dve.reciprocal(rs[:, 7, :], rs[:, 6, :])
                    if k == 15: i = tt(rs[:, 8, :], rs[:, 5, :], rs[:, 7, :], ALU.mult)
                    if k == 16: i = tt(rt[:, 7], rt[:, 2], wide(rs[:, 7, :]), ALU.mult)
                    if k == 17: i = tt(rt[:, 0], rt[:, 6], wide(rs[:, 8, :]), ALU.mult)
                    if k == 18: i = tt(coef[:], rt[:, 7], rt[:, 0], ALU.add)
                    if k == 19: i = dve.tensor_copy(c_stack[:, 0:40], flat)
                    if k == 20: i = tt(c_stack[:, 40:80], flat, c_stack[:, 0:40], ALU.subtract)
                    if k == 21: i = dve.tensor_copy(c_stack[:, 80:120], c_stack[:, 0:40])
                    i.then_inc(rt_step, 1)

            def weigh(g, t):
                a = t % 2
                dve.wait_ge(e_done, 5 * g + t + 1)
                if t == 0:
                    dve.wait_ge(rt_step, 21 * g + 18)
                if t >= 2:
                    dve.wait_ge(mix_step, 15 * g + 3 * (t - 2) + 1)
                dve.tensor_tensor(prod[a][:], ps_m[:].rearrange("p (e c) -> p e c", e=E),
                                  coef[:, t, :].unsqueeze(2).broadcast_to([P, E, D]), ALU.mult).then_inc(prod_done, 1)

            def finish(g, a):
                dve.wait_ge(cb_done, g + 1)
                dve.wait_ge(mix_step, 15 * g + 15)
                dve.tensor_tensor(yall[:], ps_m[:, 0:T * D].rearrange("p (t d) -> p t d", t=T), ymix[:], ALU.add).then_inc(yall_done, 1)
                dve.wait_ge(yall_done, g + 1)
                need(dve, res_stored[a], 8 * g - 8 * a)
                dve.scalar_tensor_tensor(out=res[a][:], in0=yall[:], scalar=1.0 / UP, in1=x1[a][:],
                                         op0=ALU.mult, op1=ALU.add).then_inc(res_done, 1)

            def step(n, a, do):
                att, wo, ex, fin, more = do
                b = 1 - a
                for r in range(RG):
                    g1, r1, on1 = back(n, r, 1, do)
                    g2, r2, on2 = back(n, r, 2, do)
                    g3, r3, on3 = back(n, r, 3, do)
                    if att: row_max(n, r, 0)
                    if r == 0 and fin: route(n - 3, range(13, 15))
                    if r == 1 and fin: weigh(n - 3, 0)
                    if r == 2 and fin: weigh(n - 3, 4)
                    if r == 3 and ex: route(n - 2, range(1, 4))
                    if on1: norm_rest(g1, r1)
                    if r == 0 and ex: sum_squares(n - 2, a, T, sq2_done, ln2P, ln2S)
                    if on2: turn_rest(g2, r2)
                    if r == 0 and att: y_low(n, 1, 0)
                    if r == 1 and att: y_low(n, 1, 3)
                    if r == 2 and more: y_low(n + 1, 0, 1)
                    if r == 3 and fin: finish(n - 3, b)
                    if r == 3 and ex: route(n - 2, range(4, 7))
                    if att: row_max(n, r, 1)
                    if r == 0 and fin: route(n - 3, range(15, 17))
                    if r == 0 and att: keep_v_rest(n, a)
                    if r == 1 and fin: weigh(n - 3, 1)
                    if r == 3 and ex: route(n - 2, range(7, 10))
                    if r == 0 and att: y_low(n, 1, 1)
                    if r == 2 and more: y_low(n + 1, 0, 2)
                    if r == 0 and fin: route(n - 3, range(17, 20))
                    if r == 1 and fin: weigh(n - 3, 2)
                    if r == 1 and ex: low(n - 2, a, T, hi2_ready, lo2_ready)
                    if on3: gated(g3, r3, a if r == 3 else b)
                    if r == 0 and att: y_low(n, 1, 2)
                    if r == 1 and more: y_low(n + 1, 0, 0)
                    if r == 2 and more: y_low(n + 1, 0, 3)
                    if r == 0 and fin: route(n - 3, range(20, 22))
                    if r == 1 and fin: weigh(n - 3, 3)
                    if r == 2 and ex: route(n - 2, range(0, 1))
                    if r == 3 and ex: route(n - 2, range(10, 13))
                    if r == 3 and wo: attention_out(n - 1, b)

            for h in range(H):
                y_low(0, 0, h)
            run_steps(dve, step)

        @KE.tensor
        def _(pe):
            mm = pe.matmul
            def turn(slabs, a, banks):
                for t in range(slabs):
                    last = pe.transpose(banks[t // T][:, P * (t % T):P * (t % T) + P],
                                        hl[a][:, t, :, :].rearrange("p s d -> p (s d)"), ident16[:])
                return last

            def bias_of(m, a):
                need(pe, b_evac, m - 1)
                pe.wait_ge(xs_made, m + 1)
                for k in range(2):
                    for r in range(RG):
                        cols = xs_pair[a][:, N * (RG * k + r):N * (RG * k + r) + N]
                        o = ps_bias[a][32 * r:32 * r + 32, N * k:N * k + N]
                        mm(o, lhsT=wb[:, 0, :], rhs=cols, start=True, stop=False)
                        last = mm(o, lhsT=wb[:, 1, :], rhs=cols, start=False, stop=True)
                last.then_inc(b_done, 1)

            def y_weights():
                pe.wait_ge(w_loaded, 16 * N_WLOAD)
                for h in range(H):
                    need(pe, gprod_done, h)
                    mm(ps_scores[1][0][:, P * h:P * h + P], lhsT=qk_raw[32 * h:32 * h + 32, 0, :],
                       rhs=qk_raw[32 * h:32 * h + 32, 1, :], start=True, stop=True).then_inc(gprod_done, 1)
            def phase1(n, a, do):
                if not do[0] and do[1]: y_weights()
                if do[3]: bias_of(n - 3, 1 - a)
                if do[2]:
                    need(pe, xs_made, n - 3)
                    pe.wait_ge(lo_ready, n - 1)
                    turn(T2, a, turned16[a]).then_inc(t1_done, 1)

            pe.wait_ge(wb_ready, 1)
            run_phase1(pe, phase1)

            pe.wait_ge(w_ready, 1)

            def y_of(g, c, h, a):
                i = 8 * g + 4 * c + h
                if c == 0 and h == 0:
                    pe.wait_ge(xs_loaded[a], 16 * g + 32 - 16 * a)
                need(pe, ylo_done, i)
                cols = xs[a][:, CH * c:CH * c + CH]
                mm(ps_y[:, 0:CH], lhsT=g_hi[:, h, :], rhs=cols, start=True, stop=False)
                mm(ps_y[:, 0:CH], lhsT=g_lo[:, h, :], rhs=cols, start=False, stop=True).then_inc(y_done, 1)

            def scores(n, r, u, a):
                q, c, off = 4 * n + r, r // 2, (r % 2) * N
                pe.wait_ge(ylo_done, 8 * n + 4 * c + 4)
                need(pe, exp_done, 2 * q + u + 1 - 4)
                full, part = xs[a][:, N * r:N * r + N], xs_mask[a][:, N * r:N * r + N]
                for k in ((0, 1, 2), (3,))[u]:
                    o = ps_scores[r % 2][u][:, (k % 3) * N:(k % 3) * N + N]
                    mm(o, lhsT=y_hi[c][:, k, off:off + P], rhs=full, start=True, stop=False)
                    mm(o, lhsT=y_lo[c][:, k, off:off + P], rhs=part, start=False, stop=False)
                    mm(o, lhsT=ident16[:], rhs=bias_hi[:, k, :], start=False, stop=False)
                    last = mm(o, lhsT=ident16[:], rhs=bias_lo[:, k, :], start=False, stop=True)
                if u == 1:
                    for h in range(H):
                        o = ps_scores[r % 2][1][32 * h:32 * h + 32, N:2 * N]
                        mm(o, lhsT=y_hi[c][:, h, off + P:off + N], rhs=full, start=True, stop=False)
                        mm(o, lhsT=y_lo[c][:, h, off + P:off + N], rhs=part, start=False, stop=False)
                    o = ps_scores[r % 2][1][:, N:2 * N]
                    mm(o, lhsT=ident16[:], rhs=bias_hi[:, H, :], start=False, stop=False)
                    last = mm(o, lhsT=ident16[:], rhs=bias_lo[:, H, :], start=False, stop=True)
                last.then_inc(s_done, 1)

            def alpha(n, r):
                q, a = 4 * n + r, r % 2
                pe.wait_ge(pnm_done, q + 1)
                need(pe, ptm_done, q)
                for h in range(H):
                    last = pe.transpose(ps_pt[:, P * h:P * h + P], pn_main[a][:, h, :], ident[:])
                last.then_inc(alpha_done, 1)

            def beta(n, r):
                q, a = 4 * n + r, r % 2
                pe.wait_ge(pnr_done, 2 * q + 2)
                need(pe, ptb_done, 2 * q)
                need(pe, og_done, q - 1)
                pe.transpose(ps_o[:, N:N + P], pn_pack[a][:, 0:P], ident[:])
                pe.transpose(ps_o[:, N + P:N + 2 * P], pn_rest[a][:].rearrange("i h j -> i (h j)"), ident[:]).then_inc(beta_done, 1)

            def attend(n, r, a, more_beta):
                q, b = 4 * n + r, r % 2
                pe.wait_ge(ptm_done, q + 1)
                pe.wait_ge(tr_done, q + 1)
                if more_beta:
                    pe.wait_ge(ptb_done, 2 * q + 4)
                else:
                    pe.wait_ge(ptb_done, 2 * q + 2)
                pe.wait_ge(v_evac, n + 1)
                pe.wait_ge(vr_evac, n + 1)
                need(pe, og_done, q)
                for h in range(H):
                    mm(ps_o[32 * h:32 * h + 32, 0:N], lhsT=v_main[a][:, r, 32 * h:32 * h + 32], rhs=pt_main[b][:, h, :],
                       start=True, stop=False)
                mm(ps_o[:, 0:N], lhsT=v_bd[a][:, r].rearrange("j h e -> j (h e)"), rhs=pt_pack[b][:], start=False, stop=True).then_inc(av_done, 1)

            reader = [None, 0]

            def take_m(sem_, value):
                if reader[0] is not None:
                    need(pe, *reader)
                reader[:] = sem_, value

            def project_v(n, a):
                take_m(v_evac, n + 1)
                for r in range(RG):
                    cols = xs[a][:, N * r:N * r + P]
                    mm(ps_m[:, P * r:P * r + P], lhsT=cols, rhs=w_hi[:, V0:V0 + P], start=True, stop=False)
                    last = mm(ps_m[:, P * r:P * r + P], lhsT=cols, rhs=w_lo[:, V0:V0 + P], start=False, stop=True)
                last.then_inc(v_done, 1)

            def project_v_rest(n, a):
                take_m(vr_evac, n + 1)
                for r in range(RG):
                    cols = xs[a][:, N * r + P:N * r + N]
                    for h in range(H):
                        o = ps_m[32 * h:32 * h + 32, DH * r:DH * r + DH]
                        mm(o, lhsT=cols, rhs=w_hi[:, V0 + DH * h:V0 + DH * h + DH], start=True, stop=False)
                        last = mm(o, lhsT=cols, rhs=w_lo[:, V0 + DH * h:V0 + DH * h + DH], start=False, stop=True)
                last.then_inc(vr_done, 1)

            def project_gate(n, a, c):
                take_m(g_evac, 2 * n + c + 1)
                cols = xs[a][:, CH * c:CH * c + CH]
                mm(ps_m[:, 0:CH], lhsT=w_hi[:, G0:G0 + P], rhs=cols, start=True, stop=False)
                mm(ps_m[:, 0:CH], lhsT=w_lo[:, G0:G0 + P], rhs=cols, start=False, stop=True).then_inc(g_done, 1)

            def turn2(g, a):
                take_m(xs2_done, g + 1)
                pe.wait_ge(lo2_ready, g + 1)
                turn(T, a, [ps_m16]).then_inc(t2_done, 1)

            def router(g):
                take_m(lg_done, g + 1)
                pe.wait_ge(xs2_done, g + 1)
                for t in range(T):
                    mm(ps_m[:, E * t:E * t + E], lhsT=xs2[:, t, :], rhs=w_hi[:, R0:R0 + E], start=True, stop=False)
                    last = mm(ps_m[:, E * t:E * t + E], lhsT=xs2[:, t, :], rhs=w_lo[:, R0:R0 + E], start=False, stop=True)
                last.then_inc(rt_done, 1)

            def project_out(g):
                take_m(x1_done, g + 1)
                pe.wait_ge(ogl_done, 4 * g + 4)
                for t in range(T):
                    o = ps_m[:, D * t:D * t + D]
                    mm(o, lhsT=og_hi[:, t:TG:T], rhs=w_hi[:, O0:O0 + D], start=True, stop=False)
                    mm(o, lhsT=og_hi[:, t:TG:T], rhs=w_lo[:, O0:O0 + D], start=False, stop=False)
                    last = mm(o, lhsT=og_lo[:, t:TG:T], rhs=w_hi[:, O0:O0 + D], start=False, stop=True)
                last.then_inc(wo_done, 1)

            def experts(g, t):
                take_m(prod_done, 5 * g + t + 1)
                mm(ps_m[:], lhsT=xs2[:, t, :], rhs=w_hi[:, X0:X0 + 512], start=True, stop=False)
                mm(ps_m[:], lhsT=xs2[:, t, :], rhs=w_lo[:, X0:X0 + 512], start=False, stop=True).then_inc(e_done, 1)

            def turn_coef(g):
                take_m(ct_evac, g + 1)
                pe.wait_ge(rt_step, 21 * g + 21)
                pe.transpose(ps_m16[:, 0:P], c_stack[:], ident16[:]).then_inc(ct_done, 1)

            def expert_bias(g):
                take_m(yall_done, g + 1)
                pe.wait_ge(ct_evac, g + 1)
                for t in range(T):
                    last = mm(ps_m[:, D * t:D * t + D], lhsT=c_t[:], rhs=eb_sel[:, t, :], start=True, stop=True)
                last.then_inc(cb_done, 1)

            def step(n, a, do):
                att, wo, ex, fin, more = do
                b = 1 - a
                if isinstance(n, int) and n == 1:
                    reader[:] = g_evac, 2 * n
                elif isinstance(n, int) and n == GROUPS + 2:
                    reader[:] = yall_done, n - 3
                elif not isinstance(n, int) or n > 1:
                    reader[:] = x1_done, n - 1
                for r in range(RG):
                    g2, r2, on2 = back(n, r, 2, do)
                    g3, r3, on3 = back(n, r, 3, do)
                    if att: scores(n, r, 0, a)
                    if r == 0 and att: project_v(n, a)
                    if r == 1 and fin: experts(n - 3, 0)
                    if r == 2 and fin: experts(n - 3, 4)
                    if r == 3 and fin: expert_bias(n - 3)
                    if r == 0 and att: y_of(n, 1, 0, a)
                    if r == 1 and att: y_of(n, 1, 3, a)
                    if r == 2 and more: y_of(n + 1, 0, 1, b)
                    if att: scores(n, r, 1, a)
                    if r == 0 and att: project_v_rest(n, a)
                    if r == 1 and fin: experts(n - 3, 1)
                    if r == 2 and ex: turn2(n - 2, a)
                    if on2: alpha(g2, r2)
                    if r == 0 and att: y_of(n, 1, 1, a)
                    if r == 2 and more: y_of(n + 1, 0, 2, b)
                    if on2: beta(g2, r2)
                    if r == 0 and att: project_gate(n, a, 0)
                    if r == 1 and fin: experts(n - 3, 2)
                    if r == 2 and fin: turn_coef(n - 3)
                    if on3: attend(g3, r3, a if r == 3 else b, on2)
                    if r == 0 and att: y_of(n, 1, 2, a)
                    if r == 1 and more: y_of(n + 1, 0, 0, b)
                    if r == 2 and more: y_of(n + 1, 0, 3, b)
                    if r == 0 and att: project_gate(n, a, 1)
                    if r == 1 and fin: experts(n - 3, 3)
                    if r == 2 and ex: router(n - 2)
                    if r == 3 and wo: project_out(n - 1)

            for h in range(H):
                y_of(0, 0, h, 0)
            pe.wait_ge(b_ready, 1)
            run_steps(pe, step)


_INS = ["x", "WqT", "WkT", "Wv", "Wg", "Wo", "Wb", "router_w", "router_b", "expert_w", "expert_b", "mask"]


def kernel(x, L0_conv_mask, L0_conv_Wq, L0_conv_Wk, L0_conv_Wv, L0_conv_Wg, L0_conv_Wo, L0_conv_Wb,
           L0_ffn_router_w, L0_ffn_router_b, L0_ffn_expert_w, L0_ffn_expert_b):
    import numpy as np
    import concourse.bacc as bacc
    from concourse.bass_utils import run_bass_kernel_spmd

    turned = lambda w: np.concatenate([np.asarray(w).T, np.asarray(w).T], axis=1)
    given = {"x": x, "WqT": turned(L0_conv_Wq), "WkT": turned(L0_conv_Wk), "Wv": L0_conv_Wv, "Wg": L0_conv_Wg,
             "Wo": L0_conv_Wo, "Wb": L0_conv_Wb, "router_w": L0_ffn_router_w, "router_b": L0_ffn_router_b,
             "expert_w": L0_ffn_expert_w, "expert_b": L0_ffn_expert_b, "mask": np.asarray(L0_conv_mask).view(np.uint8)}
    nc = bacc.Bacc("TRN2", target_bir_lowering=False, num_devices=1)
    arrays, args = {}, []
    for name in _INS:
        a = np.ascontiguousarray(given[name])
        arrays[f"in_{name}"] = a
        args.append(nc.dram_tensor(f"in_{name}", a.shape, mybir.dt.from_np(a.dtype), kind="ExternalInput").ap())
    out = nc.dram_tensor("out_0", np.asarray(x).shape, F32, kind="ExternalOutput").ap()
    build(nc, *args, out)
    r = run_bass_kernel_spmd(nc, [arrays], core_ids=[0])
    return r.results[0]["out_0"]
```

```python
from contextlib import ExitStack

import concourse.bass as bass
from concourse import mybir

ALU = mybir.AluOpType
ACT = mybir.ActivationFunctionType
AX = mybir.AxisListType
F32 = mybir.dt.float32
F16 = mybir.dt.float16

P = 128
N = 160
D = 64
H = 4
DH = 32
E = 8
RG = 4
TG = RG * N
T = TG // P
GROUPS = N // RG
PAIRS = GROUPS // 2
T2 = 2 * T
REST = N - P
CH = TG // 2
NT = H + 1
UP = 16.0
SCALE = DH ** -0.5
EPS1, EPS2 = 1e-6, 1e-5
FAR = 1e30
ROOT_D = float(D) ** 0.5


def need(eng, sem, value):
    if isinstance(value, int) and value <= 0:
        return
    eng.wait_ge(sem, value)


def build(nc, x, WqT, WkT, Wv, Wg, Wo, Wb, router_w, router_b, expert_w, expert_b, mask, out):
    with ExitStack() as ctx:
        def sb(name, shape, dt=F32):
            return ctx.enter_context(nc.sbuf_tensor(name, shape, dt))

        def sem(name):
            return ctx.enter_context(nc.semaphore(name))

        ps_scores = [[ctx.enter_context(nc.psum_tensor(f"ps_scores{a}{b}", [P, 512], F32))
                      for b in range(2)] for a in range(2)]
        ps_y = ctx.enter_context(nc.psum_tensor("ps_y", [P, 512], F32))
        ps_pt = ctx.enter_context(nc.psum_tensor("ps_pt", [P, 512], F32))
        ps_o = ctx.enter_context(nc.psum_tensor("ps_o", [P, 512], F32))
        ps_m = ctx.enter_context(nc.psum_tensor("ps_m", [P, 512], F32))
        ps_m16 = ps_m[:].bitcast(F16)
        turned16 = [[ps_m16, ps_pt[:].bitcast(F16)], [ps_scores[0][k][:].bitcast(F16) for k in range(2)]]
        ps_bias = [ps_y, ps_o]

        ident = sb("ident", [P, P])
        ident16 = sb("ident16", [P, P], F16)
        headmask = sb("headmask", [P, H])
        half = sb("half", [P, T2])
        eps1, eps2 = sb("eps1", [P, T2]), sb("eps2", [P, T2])
        order = sb("order", [P, T, E])
        w_raw = sb("w_raw", [P, 844])
        w_hi = sb("w_hi", [P, 844], F16)
        w_lo = sb("w_lo", [P, 844], F16)
        qk_raw = sb("qk_raw", [P, 2, P])
        g_hi = sb("g_hi", [P, H, P], F16)
        g_lo = sb("g_lo", [P, H, P], F16)
        rb = sb("rb", [P, T, E])
        eb_raw = sb("eb_raw", [P, T, D])
        eb_hi = sb("eb_hi", [P, T, D], F16)
        eb_diff = sb("eb_diff", [P, T, D])
        eb_sel = sb("eb_sel", [P, T, D], F16)
        is_lo = sb("is_lo", [P, 2])
        bias32 = sb("bias32", [P, NT, N])
        bias_hi = sb("bias_hi", [P, NT, N], F16)
        bias_lo = sb("bias_lo", [P, NT, N], F16)
        V0, G0, X0, R0, B0, O0 = 0, 128, 256, 768, 776, 780

        xin = [sb(f"xin{a}", [P, T2, D]) for a in range(2)]
        ln_s = [sb(f"ln_s{a}", [P, 4, T2]) for a in range(2)]
        xc = [sb(f"xc{a}", [P, T2, D]) for a in range(2)]
        sq = [sb(f"sq{a}", [P, T2, D]) for a in range(2)]
        xn = [sb(f"xn{a}", [P, T2, D]) for a in range(2)]
        hl = [sb(f"hl{a}", [P, T2, 2, D], F16) for a in range(2)]
        ln_v = [sb(f"ln_v{a}", [P, T2]) for a in range(2)]
        xs_pair = [sb(f"xs_pair{a}", [P, 2 * TG], F16) for a in range(2)]
        xs_all = sb("xs_all", [P, GROUPS * TG], F16)
        wb = sb("wb", [P, 2, 32], F16)
        mask_u8 = sb("mask_u8", [P, N], mybir.dt.uint8)
        pen = sb("pen", [P, N])
        xs_mask = [sb(f"xs_mask{a}", [P, TG], F16) for a in range(2)]
        b_stage = [sb(f"b_stage{a}", [P, 2, N]) for a in range(2)]
        xs = [sb(f"xs{a}", [P, TG], F16) for a in range(2)]
        y_hi = [sb(f"y_hi{c}", [P, H, CH], F16) for c in range(2)]
        y_lo = [sb(f"y_lo{c}", [P, H, CH], F16) for c in range(2)]
        v_main = [sb(f"v_main{a}", [P, RG, P]) for a in range(2)]
        v_bd = [sb(f"v_bd{a}", [P, RG, H, DH]) for a in range(2)]
        gate = [sb(f"gate{a}", [P, TG]) for a in range(2)]
        negmax = [sb(f"negmax{a}", [P, NT]) for a in range(2)]
        psum_row = [sb(f"psum_row{a}", [P, NT]) for a in range(2)]
        rinv = [sb(f"rinv{a}", [P, NT]) for a in range(2)]
        probs = [sb(f"probs{a}", [P, NT, N]) for a in range(2)]
        pn_main = [sb(f"pn_main{a}", [P, H, P]) for a in range(2)]
        pn_rest = [sb(f"pn_rest{a}", [P, H, REST]) for a in range(2)]
        pn_pack = [sb(f"pn_pack{a}", [P, N]) for a in range(2)]
        pt_main = [sb(f"pt_main{a}", [P, H, N]) for a in range(2)]
        pt_pack = [sb(f"pt_pack{a}", [P, N]) for a in range(2)]
        og = sb("og", [P, TG])
        og_hi = sb("og_hi", [P, TG], F16)
        og_lo = sb("og_lo", [P, TG], F16)
        x1 = [sb(f"x1_{a}", [P, T, D]) for a in range(2)]
        xs2 = sb("xs2", [P, T, P], F16)
        lg = sb("lg", [P, T, E])
        rt = sb("rt", [P, 8, T, E])
        rs = sb("rs", [P, 12, T])
        coef = sb("coef", [P, T, E])
        c_stack = sb("c_stack", [P, P], F16)
        c_t = sb("c_t", [P, P], F16)
        prod = [sb(f"prod{a}", [P, 8, D]) for a in range(2)]
        add1 = [sb(f"add1{a}", [P, 4, D]) for a in range(2)]
        add2 = [sb(f"add2{a}", [P, 2, D]) for a in range(2)]
        ymix = sb("ymix", [P, T, D])
        base = sb("base", [P, T, D])
        res = [sb(f"res{a}", [P, T, D]) for a in range(2)]

        b_dram = nc.dram_tensor("bias_scratch", [N, 32, N], F32, kind="Internal").ap()

        wb_loaded, w_loaded, const_ready = sem("wb_loaded"), sem("w_loaded"), sem("const_ready")
        wprep, wb_ready, gprod_done, w_ready = sem("wprep"), sem("wb_ready"), sem("gprod_done"), sem("w_ready")
        x_loaded = [sem(f"x_loaded{a}") for a in range(2)]
        sq_done, sq2_done = sem("sq_done"), sem("sq2_done")
        lnA, lnP, lnS, hi_ready, lo_ready = sem("lnA"), sem("lnP"), sem("lnS"), sem("hi_ready"), sem("lo_ready")
        t1_done, xs_made, b_done, b_evac = sem("t1_done"), sem("xs_made"), sem("b_done"), sem("b_evac")
        xs_kept = [sem(f"xs_kept{a}") for a in range(2)]
        b_written = [sem(f"b_written{a}") for a in range(2)]
        b_loaded, b_ready = [sem(f"b_loaded{k}") for k in range(2)], sem("b_ready")
        xs_loaded = [sem(f"xs_loaded{a}") for a in range(2)]
        y_done, yhi_done, ylo_done = sem("y_done"), sem("yhi_done"), sem("ylo_done")
        s_done, max_done, exp_done = sem("s_done"), sem("max_done"), sem("exp_done")
        rinv_done, pnm_done, pnr_done = sem("rinv_done"), sem("pnm_done"), sem("pnr_done")
        pnp_done, tr_done = sem("pnp_done"), sem("tr_done")
        alpha_done, beta_done, ptm_done, ptb_done = sem("alpha_done"), sem("beta_done"), sem("ptm_done"), sem("ptb_done")
        v_done, v_evac, vr_done, vr_evac = sem("v_done"), sem("v_evac"), sem("vr_done"), sem("vr_evac")
        g_done, g_evac = sem("g_done"), sem("g_evac")
        av_done, og_done, ogh_done, ogl_done = sem("av_done"), sem("og_done"), sem("ogh_done"), sem("ogl_done")
        wo_done, x1_done = sem("wo_done"), sem("x1_done")
        ln2A, ln2P, ln2S, xc2_done = sem("ln2A"), sem("ln2P"), sem("ln2S"), sem("xc2_done")
        hi2_ready, lo2_ready = sem("hi2_ready"), sem("lo2_ready")
        t2_done, xs2_done = sem("t2_done"), sem("xs2_done")
        rt_done, lg_done, rt_step, rt_exp = sem("rt_done"), sem("lg_done"), sem("rt_step"), sem("rt_exp")
        ct_done, ct_evac = sem("ct_done"), sem("ct_evac")
        e_done, prod_done, mix_step, mixed_last, cb_done, res_done = (
            sem("e_done"), sem("prod_done"), sem("mix_step"), sem("mixed_last"), sem("cb_done"), sem("res_done"))
        res_stored = [sem(f"res_stored{a}") for a in range(2)]

        x_flat = x.rearrange("a r j d -> (a r j d)")
        out_flat = out.rearrange("a r j d -> (a r j d)")
        b_flat = b_dram.rearrange("r h j -> (r h j)")
        tokens = lambda flat, start: flat[bass.ds(start, TG * D)].rearrange("(p t d) -> p t d", p=P, t=T)
        KE = ctx.enter_context(nc.Block())

        def pairs_loop(eng, body, first, end):
            with eng.Fori(0, (end - first) // 2) as i:
                body(i * 2 + first, first % 2)
                body(i * 2 + (first + 1), 1 - first % 2)

        N_CONST = 16 + 1 + 2

        def run_phase1(eng, step):
            for n in range(5):
                step(n, n % 2, (1, n >= 1, n >= 2, n >= 3))
            pairs_loop(eng, lambda n, a: step(n, a, (1, 1, 1, 1)), 5, PAIRS - 1)
            for n in range(PAIRS - 1, PAIRS + 3):
                step(n, n % 2, (n < PAIRS, n - 1 < PAIRS, n - 2 < PAIRS, n - 3 < PAIRS))

        def run_steps(eng, step):
            step(0, 0, (1, 0, 0, 0, 1))
            step(1, 1, (1, 1, 0, 0, 1))
            step(2, 0, (1, 1, 1, 0, 1))
            pairs_loop(eng, lambda n, a: step(n, a, (1, 1, 1, 1, 1)), 3, GROUPS - 1)
            step(GROUPS - 1, 1, (1, 1, 1, 1, 0))
            step(GROUPS, 0, (0, 1, 1, 1, 0))
            step(GROUPS + 1, 1, (0, 0, 1, 1, 0))
            step(GROUPS + 2, 0, (0, 0, 0, 1, 0))

        first_y = [ps_y, ps_scores[1][1], ps_pt, ps_m]

        def expert_bank(t, busy):
            return ps_m if busy or t % 2 == 0 else ps_scores[0][0]

        N_WLOAD = 2 * 4 + 3 + T + 3 * T + 1

        @KE.sync
        def _(sp):
            def at(g, size):
                return g * size if isinstance(g, int) else sp.snap(g * size)

            def load_x(m, a):
                start = at(m, 2 * TG * D)
                need(sp, lnA, 3 * m - 3)
                sp.dma_start(xin[a][:], x_flat[bass.ds(start, 2 * TG * D)].rearrange("(p t d) -> p t d", p=P, t=T2)
                             ).then_inc(x_loaded[a], 16)

            def keep_xs(m, a):
                start = at(m, 2 * TG)
                sp.wait_ge(xs_made, m + 1)
                sp.dma_start(xs_all[:, bass.ds(start, 2 * TG)], xs_pair[a][:]).then_inc(xs_kept[a], 16)

            def store_bias(m, a):
                start = at(m, 2 * P * N)
                sp.wait_ge(b_evac, m + 1)
                sp.dma_start(b_flat[bass.ds(start, 2 * P * N)].rearrange("(k p j) -> p k j", k=2, p=P), b_stage[a][:]
                             ).then_inc(b_written[a], 16)

            for m in range(2):
                load_x(m, m)
            for half_ in range(2):
                sp.dma_start(w_raw[64 * half_:64 * half_ + 64, B0:B0 + 4], Wb).then_inc(wb_loaded, 16)
            ld = lambda dst, src: sp.dma_start(dst, src).then_inc(w_loaded, 16)
            for half_ in range(2):
                rows = slice(64 * half_, 64 * half_ + 64)
                ld(w_raw[rows, V0:V0 + 128], Wv)
                ld(w_raw[rows, G0:G0 + 128], Wg)
                ld(w_raw[rows, X0:X0 + 512].rearrange("p (e c) -> p e c", e=E), expert_w.rearrange("e d c -> d e c"))
                ld(w_raw[rows, R0:R0 + 8], router_w)
                load_x(2 + half_, half_)
            ld(w_raw[:, O0:O0 + 64], Wo)
            ld(qk_raw[:, 0, :], WqT)
            ld(qk_raw[:, 1, :], WkT)
            ld(mask_u8[D:P, :], mask.broadcast_to([P - D, N]))
            load_x(4, 0)
            for t in range(T):
                ld(rb[:, t, :], router_b.rearrange("(a e) -> a e", a=1).broadcast_to([P, E]))
            load_x(5, 1)
            keep_xs(0, 0)
            keep_xs(1, 1)
            store_bias(0, 0)
            load_x(6, 0)
            sp.wait_ge(const_ready, 1)

            def load_eb(part):
                for t in range(T):
                    ld(eb_raw[40 * part + 8 * t:40 * part + 8 * t + 8, t, :], expert_b)

            load_eb(0)
            keep_xs(2, 0)
            store_bias(1, 1)
            load_x(7, 1)
            load_eb(1)
            keep_xs(3, 1)
            store_bias(2, 0)
            load_eb(2)

            def load_xs(g, a):
                start = at(g, TG)
                need(sp, s_done, 8 * (g - 1))
                sp.dma_start(xs[a][:], xs_all[:, bass.ds(start, TG)]).then_inc(xs_loaded[a], 16)
                sp.dma_start(xs_mask[a][0:D, :], xs_all[0:D, bass.ds(start, TG)]).then_inc(xs_loaded[a], 16)

            def phase1(n, a):
                load_x(n + 1, 1 - a)
                keep_xs(n - 3, 1 - a)
                store_bias(n - 4, a)

            pairs_loop(sp, phase1, 7, PAIRS - 1)
            for n in range(PAIRS - 1, PAIRS + 4):
                if n + 1 < PAIRS: load_x(n + 1, 1 - n % 2)
                if n - 3 < PAIRS: keep_xs(n - 3, 1 - n % 2)
                store_bias(n - 4, n % 2)
                if n == PAIRS:
                    sp.wait_ge(xs_kept[0], 16)
                    for g in range(2):
                        load_xs(g, g)
                if n == PAIRS + 1:
                    for a in range(2):
                        sp.wait_ge(b_written[a], 16 * (P // (2 * RG) // 2))
                    sp.dma_start(bias32[:, 0:H, :], b_dram[0:P, 0:H, :]).then_inc(b_loaded[0], 16)

            for a in range(2):
                sp.wait_ge(b_written[a], 16 * (PAIRS // 2))
            for h in range(H):
                sp.dma_start(bias32[32 * h:32 * h + 32, H, :], b_dram[P:N, h, :]).then_inc(b_loaded[1], 16)

            def load_res(g, a):
                start = at(g, TG * D)
                need(sp, x1_done, g - 1)
                sp.dma_start(xin[a][:, 0:T], tokens(x_flat, start)).then_inc(x_loaded[a], 16)

            def store(g, a):
                start = at(g, TG * D)
                sp.wait_ge(res_done, g + 1)
                sp.dma_start(tokens(out_flat, start), res[a][:]).then_inc(res_stored[a], 16)

            for a in range(2):
                sp.wait_ge(xs_kept[a], 16 * (PAIRS // 2))
            for g in range(2):
                load_res(g, g)

            def phase2(g, a):
                load_xs(g, a)
                load_res(g, a)
                store(g - 4, a)

            for g in range(2, 4):
                load_xs(g, g % 2)
                load_res(g, g % 2)
            pairs_loop(sp, phase2, 4, GROUPS)
            for g in range(GROUPS - 4, GROUPS):
                store(g, g % 2)
            for a in range(2):
                sp.wait_ge(res_stored[a], 16 * (GROUPS // 2))

        @KE.gpsimd
        def _(pool):
            pool.memset(eb_raw[:], 0.0).then_inc(const_ready, 1)
            pool.memset(ident[:], 0.0).then_inc(const_ready, 1)
            pool.memset(headmask[:], 0.0).then_inc(const_ready, 1)
            pool.memset(half[:], -0.5).then_inc(const_ready, 1)
            pool.memset(eps1[:], EPS1).then_inc(const_ready, 1)
            pool.memset(eps2[:], EPS2).then_inc(const_ready, 1)
            pool.memset(c_stack[:], 0.0).then_inc(const_ready, 1)
            pool.memset(is_lo[:], 0.0).then_inc(const_ready, 1)
            for e in range(E):
                pool.memset(order[:, :, e], float(E - e)).then_inc(const_ready, 1)
            pool.wait_ge(const_ready, 16)
            pool.affine_select(out=ident[:], in_=ident[:], compare_op=ALU.not_equal, fill=1.0, base=0,
                               pattern=[[-1, P]], channel_multiplier=1).then_inc(const_ready, 1)
            pool.affine_select(out=is_lo[:, 0:1], in_=is_lo[:, 0:1], compare_op=ALU.is_gt, fill=1.0, base=80,
                               pattern=[[0, 1]], channel_multiplier=-1).then_inc(const_ready, 1)
            pool.affine_select(out=is_lo[:, 1:2], in_=is_lo[:, 1:2], compare_op=ALU.is_ge, fill=1.0, base=-80,
                               pattern=[[0, 1]], channel_multiplier=1).then_inc(const_ready, 1)

            def ln_scale(g, a, w, sums, step, eps, own):
                pool.wait_ge(sums, g + 1)
                pool.tensor_tensor(ln_v[a][:, 0:w], ln_s[a][:, 2, 0:w], eps[:, 0:w], ALU.add).then_inc(own, 1)
                pool.wait_ge(own, 3 * g + 1)
                pool.tensor_tensor(ln_s[a][:, 3, 0:w], ln_v[a][:, 0:w], half[:, 0:w], ALU.pow).then_inc(own, 1)
                pool.wait_ge(own, 3 * g + 2)
                need(pool, step, g - 1)
                pool.tensor_tensor(xn[a][:, 0:w], xc[a][:, 0:w], ln_s[a][:, 3, 0:w].unsqueeze(2).broadcast_to([P, w, D]),
                                   ALU.mult).then_inc(own, 1)

            def phase1(n, a, do):
                if do[1]: ln_scale(n - 1, 1 - a, T2, lnS, lo_ready, eps1, lnP)

            run_phase1(pool, phase1)

            def norm_main(g, r):
                a = r % 2
                pool.wait_ge(rinv_done, 4 * g + r + 1)
                need(pool, beta_done, 4 * g + r - 1)
                pool.tensor_tensor(pn_main[a][:], probs[a][:, 0:H, 0:P],
                                   rinv[a][:, 0:H].unsqueeze(2).broadcast_to([P, H, P]), ALU.mult).then_inc(pnm_done, 1)

            def norm_rest(g, r):
                q, a = 4 * g + r, r % 2
                pool.wait_ge(rinv_done, q + 1)
                need(pool, beta_done, q - 1)
                pool.tensor_tensor(pn_rest[a][:], probs[a][:, 0:H, P:N],
                                   rinv[a][:, 0:H].unsqueeze(2).broadcast_to([P, H, REST]), ALU.mult).then_inc(pnr_done, 1)

            def center(g, a):
                pool.wait_ge(ln2A, 2 * g + 2)
                need(pool, sq2_done, g - 1)
                need(pool, ln2P, 3 * (g - 1))
                pool.tensor_tensor(xc[a][:, 0:T], x1[a][:], ln_s[a][:, 1, 0:T].unsqueeze(2).broadcast_to([P, T, D]),
                                   ALU.add).then_inc(xc2_done, 1)

            def og_low(g, r):
                pool.wait_ge(ogh_done, 4 * g + r + 1)
                pool.tensor_tensor(og_lo[:, N * r:N * r + N], og[:, N * r:N * r + N], og_hi[:, N * r:N * r + N],
                                   ALU.subtract).then_inc(ogl_done, 1)

            def mix(g, t):
                a, b = t % 2, 13 * g + 3 * t
                pool.wait_ge(prod_done, 5 * g + t + 1)
                pool.tensor_tensor(add1[a][:], prod[a][:, 0:4, :], prod[a][:, 4:8, :], ALU.add).then_inc(mix_step, 1)
                pool.wait_ge(mix_step, b + 1)
                pool.tensor_tensor(add2[a][:], add1[a][:, 0:2, :], add1[a][:, 2:4, :], ALU.add).then_inc(mix_step, 1)
                pool.wait_ge(mix_step, b + 2)
                pool.tensor_tensor(ymix[:, t, :], add2[a][:, 0, :], add2[a][:, 1, :], ALU.add).then_inc(mix_step, 1)

            def residual(g, a):
                pool.wait_ge(mix_step, 13 * g + 12)
                pool.wait_ge(mixed_last, g + 1)
                need(pool, res_done, g)
                pool.tensor_tensor(base[:], ymix[:], x1[a][:], ALU.add).then_inc(mix_step, 1)
                pool.wait_ge(mix_step, 13 * g + 13)

            def step(n, a, do):
                att, wo, ex, fin, _ = do
                if ex: center(n - 2, a)
                if wo: norm_main(n - 1, 3)
                if ex: ln_scale(n - 2, a, T, ln2S, lo2_ready, eps2, ln2P)
                if wo: norm_rest(n - 1, 3)
                if wo: og_low(n - 1, 0)
                if wo: og_low(n - 1, 1)
                if att: norm_rest(n, 0)
                if att: norm_main(n, 0)
                if fin: mix(n - 3, 0)
                if fin: mix(n - 3, 1)
                if fin: mix(n - 3, 2)
                if wo: og_low(n - 1, 2)
                if fin: mix(n - 3, 3)
                if att: norm_rest(n, 1)
                if att: norm_main(n, 1)
                if att: norm_rest(n, 2)
                if fin: residual(n - 3, 1 - a)
                if wo: og_low(n - 1, 3)
                if att: norm_main(n, 2)

            run_steps(pool, step)

        @KE.scalar
        def _(act):
            def square(g, a, w, src_done, value, sums, own):
                act.wait_ge(src_done, value)
                need(act, sums, g - 1)
                act.activation(sq[a][:, 0:w], xc[a][:, 0:w], ACT.Square, scale=1.0 / ROOT_D).then_inc(own, 1)

            def high(g, a, w, scaled, transposed, own):
                act.wait_ge(scaled, 3 * g + 3)
                need(act, transposed, g - 1)
                act.activation(hl[a][:, 0:w, 0, :], xn[a][:, 0:w], ACT.Copy).then_inc(own, 1)

            def make_xs(m, a):
                act.wait_ge(t1_done, m + 1)
                need(act, b_done, m - 1)
                need(act, xs_kept[a], 8 * m - 8 * a)
                for k in range(2):
                    i = act.activation(xs_pair[a][:].rearrange("c (p t) -> c t p", t=T2)[:, T * k:T * k + T],
                                       turned16[a][k][:, 0:TG].rearrange("c (t p) -> c t p", t=T), ACT.Copy)
                i.then_inc(xs_made, 1)

            def phase1(n, a, do):
                if do[2]: high(n - 2, a, T2, lnP, t1_done, hi_ready)
                if do[3]: make_xs(n - 3, 1 - a)
                if do[0]: square(n, a, T2, lnA, 3 * n + 3, lnS, sq_done)
                if do[3]:
                    act.wait_ge(b_done, n - 2)
                    need(act, b_written[1 - a], 8 * (n - 3) - 8 * (1 - a))
                    act.activation(b_stage[1 - a][:], ps_bias[1 - a][:, 0:2 * N].rearrange("p (k j) -> p k j", k=2),
                                   ACT.Copy, scale=1.0 / UP).then_inc(b_evac, 1)

            run_phase1(act, phase1)

            def exp(n, r, u):
                a, k0, k1 = r % 2, (0, 3)[u], (3, NT)[u]
                act.wait_ge(max_done, 8 * n + 2 * r + u + 1)
                need(act, pnm_done, 4 * n + r - 1)
                need(act, pnr_done, 4 * n + r - 1)
                for k in range(k0, k1):
                    e = act.activation(probs[a][:, k, :], ps_scores[a][u][:, (k - k0) * N:(k - k0 + 1) * N], ACT.Exp,
                                       bias=negmax[a][:, k:k + 1], accum_out=psum_row[a][:, k:k + 1])
                e.then_inc(exp_done, 1)

            def norm_pack(n, r):
                q, a = 4 * n + r, r % 2
                act.wait_ge(rinv_done, q + 1)
                need(act, beta_done, q - 1)
                need(act, tr_done, q - 1)
                act.activation(pn_pack[a][:], probs[a][:, H, :], ACT.Copy, scale=rinv[a][:, H:NT]).then_inc(pnp_done, 1)

            def pt_alpha(n, r):
                q, a = 4 * n + r, r % 2
                act.wait_ge(alpha_done, q + 1)
                need(act, av_done, q - 1)
                act.activation(pt_main[a][:, :, 0:P], ps_pt[:].rearrange("j (h i) -> j h i", h=H),
                               ACT.Copy).then_inc(ptm_done, 1)

            def pt_beta(n, r):
                q, a = 4 * n + r, r % 2
                act.wait_ge(beta_done, q + 1)
                act.activation(pt_main[a][:, :, P:N], ps_o[:, N:N + P].rearrange("j (h i) -> j h i", h=H),
                               ACT.Copy).then_inc(ptb_done, 1)
                act.activation(pt_pack[a][:, 0:P], ps_o[:, N + P:N + 2 * P], ACT.Copy).then_inc(ptb_done, 1)

            def y_high(g, c, h, bank=ps_y):
                act.wait_ge(y_done, 8 * g + 4 * c + h + 1)
                need(act, s_done, 8 * (g - 1) + 4 * (c + 1))
                act.activation(y_hi[c][:, h, :], bank[:, 0:CH], ACT.Copy, scale=1.0 / UP).then_inc(yhi_done, 1)

            def og_high(n, r):
                act.wait_ge(og_done, 4 * n + r + 1)
                need(act, wo_done, n)
                act.activation(og_hi[:, N * r:N * r + N], og[:, N * r:N * r + N], ACT.Copy).then_inc(ogh_done, 1)

            def keep_v(n, a):
                act.wait_ge(v_done, n + 1)
                need(act, av_done, 4 * (n - 1))
                act.activation(v_main[a][:], ps_m[:].rearrange("j (r e) -> j r e", r=RG), ACT.Copy,
                               scale=1.0 / UP).then_inc(v_evac, 1)

            def tanh_gate(n, a, c):
                act.wait_ge(g_done, 2 * n + c + 1)
                need(act, og_done, 4 * (n - 1))
                act.activation(gate[a][:, CH * c:CH * c + CH], ps_m[:, 0:CH], ACT.Tanh,
                               scale=0.5 / UP).then_inc(g_evac, 1)

            def keep_xs2(g):
                act.wait_ge(t2_done, g + 1)
                need(act, e_done, 5 * g)
                act.activation(xs2[:], ps_m16[:, 0:TG].rearrange("c (t p) -> c t p", t=T), ACT.Copy).then_inc(xs2_done, 1)

            def router_exp(g):
                act.wait_ge(rt_step, 19 * g + 12)
                act.activation(rs[:, 5, :], rs[:, 4, :], ACT.Exp, scale=1.0 / UP).then_inc(rt_exp, 1)

            def keep_coef(g):
                act.wait_ge(ct_done, g + 1)
                act.activation(c_t[:], ps_m16[:, 0:P], ACT.Copy).then_inc(ct_evac, 1)

            def step(n, a, do):
                att, wo, ex, fin, more = do
                if wo: exp(n - 1, 3, 1)
                if att: keep_v(n, a)
                if att: y_high(n, 1, 0)
                if ex: square(n - 2, a, T, xc2_done, n - 1, ln2S, sq2_done)
                if wo: pt_beta(n - 1, 2)
                if att: exp(n, 0, 0)
                if wo: norm_pack(n - 1, 3)
                if att: y_high(n, 1, 1)
                if wo: pt_alpha(n - 1, 2)
                if att: tanh_gate(n, a, 0)
                if att: exp(n, 0, 1)
                if att: y_high(n, 1, 2)
                if wo: og_high(n - 1, 1)
                if att: tanh_gate(n, a, 1)
                if att: y_high(n, 1, 3)
                if att: exp(n, 1, 0)
                if ex: high(n - 2, a, T, ln2P, t2_done, hi2_ready)
                if wo: pt_beta(n - 1, 3)
                if more: y_high(n + 1, 0, 0)
                if att: exp(n, 1, 1)
                if wo: og_high(n - 1, 2)
                if wo: pt_alpha(n - 1, 3)
                if att: norm_pack(n, 0)
                if more: y_high(n + 1, 0, 1)
                if att: exp(n, 2, 0)
                if ex: keep_xs2(n - 2)
                if more: y_high(n + 1, 0, 2)
                if fin: keep_coef(n - 3)
                if att: pt_beta(n, 0)
                if att: norm_pack(n, 1)
                if att: exp(n, 2, 1)
                if att: pt_alpha(n, 0)
                if more: y_high(n + 1, 0, 3)
                if att: pt_beta(n, 1)
                if wo: og_high(n - 1, 3)
                if att: norm_pack(n, 2)
                if att: exp(n, 3, 0)
                if att: pt_alpha(n, 1)
                if att: og_high(n, 0)
                if ex: router_exp(n - 2)

            for h in range(H):
                y_high(0, 0, h, first_y[h])
            run_steps(act, step)

        @KE.vector
        def _(dve):
            made = [0]

            def prep(ins):
                ins.then_inc(wprep, 1)
                made[0] += 1
                dve.wait_ge(wprep, made[0])

            for c in range(2):
                prep(dve.memset(y_lo[c][D:P, :, :], 32768.0))
            prep(dve.memset(wb[:], 0.0))
            dve.wait_ge(const_ready, N_CONST)
            for h in range(H):
                prep(dve.memset(headmask[32 * h:32 * h + 32, h:h + 1], 1.0 / UP))
            prep(dve.tensor_copy(ident16[:], ident[:]))
            dve.wait_ge(wb_loaded, 32)
            prep(dve.tensor_scalar(wb[:, 0, 0:H], w_raw[:, B0:B0 + H], UP, None, ALU.mult))
            prep(dve.scalar_tensor_tensor(out=wb[:, 1, 0:H], in0=w_raw[:, B0:B0 + H], scalar=UP, in1=wb[:, 0, 0:H],
                                          op0=ALU.mult, op1=ALU.subtract))
            dve.nop().then_inc(wb_ready, 1)

            def total(g, a, w, src, own):
                dve.tensor_reduce(ln_s[a][:, 0, 0:w], src[a][:, 0:w], AX.X, ALU.add).then_inc(own, 1)

            def mean(g, a, w, own, steps):
                dve.wait_ge(own, steps * g + 1)
                dve.tensor_scalar(ln_s[a][:, 1, 0:w], ln_s[a][:, 0, 0:w], -1.0 / D, None, ALU.mult).then_inc(own, 1)

            def center(g, a, w, src, own, used_by_square, used_by_scale):
                dve.wait_ge(own, 3 * g + 2)
                need(dve, used_by_square, g - 1)
                need(dve, used_by_scale, 3 * (g - 1))
                dve.tensor_tensor(xc[a][:, 0:w], src[a][:, 0:w], ln_s[a][:, 1, 0:w].unsqueeze(2).broadcast_to([P, w, D]),
                                  ALU.add).then_inc(own, 1)

            def sum_squares(g, a, w, squared, scaled, own):
                dve.wait_ge(squared, g + 1)
                need(dve, scaled, 3 * (g - 1))
                dve.tensor_reduce(ln_s[a][:, 2, 0:w], sq[a][:, 0:w], AX.X, ALU.add).then_inc(own, 1)

            def low(g, a, w, high_done, own):
                dve.wait_ge(high_done, g + 1)
                dve.tensor_tensor(hl[a][:, 0:w, 1, :], xn[a][:, 0:w], hl[a][:, 0:w, 0, :], ALU.subtract).then_inc(own, 1)

            def weight_halves():
                dve.wait_ge(w_loaded, 16 * N_WLOAD)
                prep(dve.tensor_scalar(w_hi[:, 0:B0], w_raw[:, 0:B0], UP, None, ALU.mult))
                prep(dve.tensor_scalar(w_hi[:, O0:O0 + D], w_raw[:, O0:O0 + D], UP, None, ALU.mult))
                prep(dve.scalar_tensor_tensor(out=w_lo[:, 0:B0], in0=w_raw[:, 0:B0], scalar=UP, in1=w_hi[:, 0:B0],
                                              op0=ALU.mult, op1=ALU.subtract))
                prep(dve.scalar_tensor_tensor(out=w_lo[:, O0:O0 + D], in0=w_raw[:, O0:O0 + D], scalar=UP, in1=w_hi[:, O0:O0 + D],
                                              op0=ALU.mult, op1=ALU.subtract))

            def y_weights():
                dve.wait_ge(gprod_done, H)
                g_of = ps_scores[1][0][:].rearrange("p (h c) -> p h c", h=H)
                prep(dve.tensor_scalar(g_hi[:], g_of, SCALE * UP, None, ALU.mult))
                prep(dve.scalar_tensor_tensor(out=g_lo[:], in0=g_of, scalar=SCALE * UP, in1=g_hi[:], op0=ALU.mult, op1=ALU.subtract))
                prep(dve.tensor_scalar(pen[D:P, :], mask_u8[D:P, :], -1.0, 65504.0, ALU.add, ALU.mult))
                for a in range(2):
                    prep(dve.tensor_copy(xs_mask[a][D:P, :].rearrange("p (r j) -> p r j", r=RG),
                                         pen[D:P, :].unsqueeze(1).broadcast_to([P - D, RG, N])))
                dve.nop().then_inc(w_ready, 1)

            def expert_bias_halves():
                prep(dve.tensor_scalar(rb[:], rb[:], UP, None, ALU.mult))
                prep(dve.tensor_scalar(eb_hi[:], eb_raw[:], UP, None, ALU.mult))
                prep(dve.scalar_tensor_tensor(out=eb_diff[:], in0=eb_raw[:], scalar=UP, in1=eb_hi[:], op0=ALU.mult, op1=ALU.subtract))
                prep(dve.tensor_scalar(eb_diff[:], eb_diff[:], is_lo[:, 0:1], None, ALU.mult))
                prep(dve.scalar_tensor_tensor(out=eb_sel[:], in0=eb_hi[:], scalar=is_lo[:, 1:2], in1=eb_diff[:],
                                              op0=ALU.mult, op1=ALU.add))

            def phase1(n, a, do):
                if do[0]:
                    dve.wait_ge(x_loaded[a], 8 * n + 16 - 8 * a)
                    total(n, a, T2, xin, lnA)
                if do[1]: sum_squares(n - 1, 1 - a, T2, sq_done, lnP, lnS)
                if do[0]: mean(n, a, T2, lnA, 3)
                if do[0]: center(n, a, T2, xin, lnA, sq_done, lnP)
                if do[2]: low(n - 2, a, T2, hi_ready, lo_ready)
                if not do[0]:
                    if n == PAIRS: weight_halves()
                    if n == PAIRS + 1: y_weights()

            run_phase1(dve, phase1)

            def y_low(g, c, h, bank=ps_y):
                i = 8 * g + 4 * c + h
                dve.wait_ge(yhi_done, i + 1)
                dve.scalar_tensor_tensor(out=y_lo[c][0:D, h, :], in0=bank[0:D, 0:CH], scalar=1.0 / UP,
                                         in1=y_hi[c][0:D, h, :], op0=ALU.mult, op1=ALU.subtract).then_inc(ylo_done, 1)

            for h in range(H):
                y_low(0, 0, h, first_y[h])
            for k, part in enumerate((slice(0, H), slice(H, NT))):
                dve.wait_ge(b_loaded[k], (16, 16 * H)[k])
                prep(dve.tensor_copy(bias_hi[:, part], bias32[:, part]))
                prep(dve.tensor_tensor(bias_lo[:, part], bias32[:, part], bias_hi[:, part], ALU.subtract))
            dve.nop().then_inc(b_ready, 1)
            expert_bias_halves()

            def row_max(n, r, u):
                a, k0, k1 = r % 2, (0, 3)[u], (3, NT)[u]
                i = 8 * n + 2 * r + u
                dve.wait_ge(s_done, i + 1)
                dve.tensor_reduce(negmax[a][:, k0:k1],
                                  ps_scores[a][u][:, 0:(k1 - k0) * N].rearrange("i (k j) -> i k j", j=N),
                                  AX.X, ALU.max, negate=True).then_inc(max_done, 1)

            def invert(n, r):
                q, a = 4 * n + r, r % 2
                dve.wait_ge(exp_done, 2 * q + 2)
                need(dve, pnm_done, q - 1)
                need(dve, pnr_done, q - 1)
                need(dve, pnp_done, q - 1)
                dve.reciprocal(rinv[a][:], psum_row[a][:]).then_inc(rinv_done, 1)

            def turn_rest(n, r):
                q, a = 4 * n + r, r % 2
                dve.wait_ge(pnp_done, q + 1)
                need(dve, av_done, q - 1)
                dve.transpose(pt_pack[a][:, P:N], pn_pack[a][:, P:N]).then_inc(tr_done, 1)

            def gated(n, r, a):
                q = 4 * n + r
                dve.wait_ge(av_done, q + 1)
                dve.wait_ge(g_evac, 2 * n + 2)
                need(dve, ogl_done, q - 3)
                dve.scalar_tensor_tensor(out=og[:, N * r:N * r + N], in0=gate[a][:, N * r:N * r + N], scalar=1.0,
                                         in1=ps_o[:, 0:N], op0=ALU.add, op1=ALU.mult).then_inc(og_done, 1)

            def keep_v_rest(n, a):
                dve.wait_ge(vr_done, n + 1)
                need(dve, av_done, 4 * (n - 1))
                dve.tensor_tensor(v_bd[a][:],
                                  ps_m[:, 0:RG * DH].rearrange("j (r e) -> j r e", r=RG).unsqueeze(2).broadcast_to([P, RG, H, DH]),
                                  headmask[:].unsqueeze(1).unsqueeze(3).broadcast_to([P, RG, H, DH]),
                                  ALU.mult).then_inc(vr_evac, 1)

            def attention_out(g, a):
                dve.wait_ge(wo_done, g + 1)
                dve.wait_ge(x_loaded[a], 4 * GROUPS + 8 * g + 16 - 8 * a)
                need(dve, res_done, g - 1)
                dve.scalar_tensor_tensor(out=x1[a][:], in0=ps_m[:, 0:T * D].rearrange("p (t d) -> p t d", t=T),
                                         scalar=0.5 / UP, in1=xin[a][:, 0:T], op0=ALU.mult, op1=ALU.add).then_inc(x1_done, 1)
                dve.wait_ge(x1_done, g + 1)
                total(g, a, T, x1, ln2A)
                mean(g, a, T, ln2A, 2)

            wide = lambda v: v.unsqueeze(2).broadcast_to([P, T, E])

            def route(g, k):
                L, tt, red = lg[:], dve.tensor_tensor, dve.tensor_reduce
                flat = coef[:].rearrange("p t e -> p (t e)")
                if k == 0:
                    dve.wait_ge(rt_done, g + 1)
                    tt(L, ps_m[:, 0:T * E].rearrange("p (t e) -> p t e", t=T), rb[:], ALU.add).then_inc(lg_done, 1)
                    return
                if k == 1:
                    dve.wait_ge(lg_done, g + 1)
                else:
                    dve.wait_ge(rt_step, 19 * g + k - 1)
                if k == 13:
                    dve.wait_ge(rt_exp, g + 1)
                if k == 1: i = red(rs[:, 0, :], L, AX.X, ALU.max)
                if k == 2: i = tt(rt[:, 0], L, wide(rs[:, 0, :]), ALU.is_equal)
                if k == 3: i = tt(rt[:, 1], rt[:, 0], order[:], ALU.mult)
                if k == 4: i = red(rs[:, 1, :], rt[:, 1], AX.X, ALU.max)
                if k == 5: i = tt(rt[:, 2], rt[:, 1], wide(rs[:, 1, :]), ALU.is_equal)
                if k == 6: i = dve.scalar_tensor_tensor(out=rt[:, 3], in0=rt[:, 2], scalar=-FAR, in1=L,
                                                        op0=ALU.mult, op1=ALU.add)
                if k == 7: i = red(rs[:, 2, :], rt[:, 3], AX.X, ALU.max)
                if k == 8: i = tt(rt[:, 4], rt[:, 3], wide(rs[:, 2, :]), ALU.is_equal)
                if k == 9: i = tt(rt[:, 5], rt[:, 4], order[:], ALU.mult)
                if k == 10: i = red(rs[:, 3, :], rt[:, 5], AX.X, ALU.max)
                if k == 11: i = tt(rt[:, 6], rt[:, 5], wide(rs[:, 3, :]), ALU.is_equal)
                if k == 12: i = tt(rs[:, 4, :], rs[:, 2, :], rs[:, 0, :], ALU.subtract)
                if k == 13: i = dve.tensor_scalar(rs[:, 6, :], rs[:, 5, :], 1.0, None, ALU.add)
                if k == 14: i = dve.reciprocal(rs[:, 7, :], rs[:, 6, :])
                if k == 15: i = tt(rt[:, 7], rt[:, 6], wide(rs[:, 5, :]), ALU.mult)
                if k == 16: i = tt(rt[:, 0], rt[:, 7], rt[:, 2], ALU.add)
                if k == 17: i = tt(coef[:], rt[:, 0], wide(rs[:, 7, :]), ALU.mult)
                if k == 18:
                    i = dve.tensor_copy(c_stack[:, 0:3 * T * E].rearrange("p (s c) -> p s c", s=3)[:, 0:3:2, :],
                                        flat.unsqueeze(1).broadcast_to([P, 2, T * E]))
                if k == 19: i = tt(c_stack[:, 40:80], flat, c_stack[:, 0:40], ALU.subtract)
                i.then_inc(rt_step, 1)

            def weigh(g, t, busy):
                a = t % 2
                dve.wait_ge(e_done, 5 * g + t + 1)
                if t == 0:
                    dve.wait_ge(rt_step, 19 * g + 17)
                if t >= 2:
                    dve.wait_ge(mix_step, 13 * g + 3 * (t - 2) + 1)
                given = expert_bank(t, busy)[:].rearrange("p (e c) -> p e c", e=E)
                dve.scalar_tensor_tensor(out=prod[a][:], in0=given, scalar=1.0 / UP,
                                         in1=coef[:, t, :].unsqueeze(2).broadcast_to([P, E, D]),
                                         op0=ALU.mult, op1=ALU.mult).then_inc(prod_done, 1)

            def mix_last(g):
                dve.wait_ge(prod_done, 5 * g + 5)
                dve.tensor_reduce(ymix[:, T - 1, :], prod[(T - 1) % 2][:].rearrange("p e c -> p c e"),
                                  AX.X, ALU.add).then_inc(mixed_last, 1)

            def finish(g, a):
                dve.wait_ge(cb_done, g + 1)
                dve.wait_ge(mix_step, 13 * g + 13)
                need(dve, res_stored[a], 8 * g - 8 * a)
                dve.scalar_tensor_tensor(out=res[a][:], in0=ps_m[:, 0:T * D].rearrange("p (t d) -> p t d", t=T), scalar=1.0 / UP,
                                         in1=base[:], op0=ALU.mult, op1=ALU.add).then_inc(res_done, 1)

            def step(n, a, do):
                att, wo, ex, fin, more = do
                b = 1 - a
                if att: row_max(n, 0, 0)
                if wo: invert(n - 1, 3)
                if fin: route(n - 3, 13)
                if att: y_low(n, 1, 0)
                if wo: turn_rest(n - 1, 2)
                if ex: sum_squares(n - 2, a, T, sq2_done, ln2P, ln2S)
                if fin: route(n - 3, 14)
                if att: keep_v_rest(n, a)
                if fin: route(n - 3, 15)
                if fin: route(n - 3, 16)
                if fin: route(n - 3, 17)
                if att: row_max(n, 0, 1)
                if att: y_low(n, 1, 1)
                if fin: route(n - 3, 18)
                if wo: gated(n - 1, 1, b)
                if fin: route(n - 3, 19)
                if att: y_low(n, 1, 2)
                if att: row_max(n, 1, 0)
                if att: invert(n, 0)
                if fin: weigh(n - 3, 0, att)
                if att: y_low(n, 1, 3)
                if fin: weigh(n - 3, 1, att)
                if att: row_max(n, 1, 1)
                if wo: turn_rest(n - 1, 3)
                if fin: weigh(n - 3, 2, att)
                if more: y_low(n + 1, 0, 0)
                if wo: gated(n - 1, 2, b)
                if fin: weigh(n - 3, 3, att)
                if ex: low(n - 2, a, T, hi2_ready, lo2_ready)
                if att: row_max(n, 2, 0)
                if fin: weigh(n - 3, 4, att)
                if att: turn_rest(n, 0)
                if more: y_low(n + 1, 0, 1)
                if fin: mix_last(n - 3)
                if att: row_max(n, 2, 1)
                if att: invert(n, 1)
                if more: y_low(n + 1, 0, 2)
                if wo: gated(n - 1, 3, b)
                if att: invert(n, 2)
                if ex: route(n - 2, 0)
                if ex: route(n - 2, 1)
                if att: row_max(n, 3, 0)
                if ex: route(n - 2, 2)
                if ex: route(n - 2, 3)
                if ex: route(n - 2, 4)
                if att: row_max(n, 3, 1)
                if ex: route(n - 2, 5)
                if more: y_low(n + 1, 0, 3)
                if ex: route(n - 2, 6)
                if fin: finish(n - 3, b)
                if ex: route(n - 2, 7)
                if att: gated(n, 0, a)
                if ex: route(n - 2, 8)
                if ex: route(n - 2, 9)
                if ex: route(n - 2, 10)
                if att: turn_rest(n, 1)
                if ex: route(n - 2, 11)
                if ex: route(n - 2, 12)
                if wo: attention_out(n - 1, b)

            run_steps(dve, step)

        @KE.tensor
        def _(pe):
            mm = pe.matmul
            def turn(slabs, a, banks):
                for t in range(slabs):
                    last = pe.transpose(banks[t // T][:, P * (t % T):P * (t % T) + P],
                                        hl[a][:, t, :, :].rearrange("p s d -> p (s d)"), ident16[:])
                return last

            def bias_of(m, a):
                need(pe, b_evac, m - 1)
                pe.wait_ge(xs_made, m + 1)
                for k in range(2):
                    for r in range(RG):
                        cols = xs_pair[a][:, N * (RG * k + r):N * (RG * k + r) + N]
                        o = ps_bias[a][32 * r:32 * r + 32, N * k:N * k + N]
                        mm(o, lhsT=wb[:, 0, :], rhs=cols, start=True, stop=False)
                        last = mm(o, lhsT=wb[:, 1, :], rhs=cols, start=False, stop=True)
                last.then_inc(b_done, 1)

            def y_weights():
                pe.wait_ge(w_loaded, 16 * N_WLOAD)
                for h in range(H):
                    need(pe, gprod_done, h)
                    mm(ps_scores[1][0][:, P * h:P * h + P], lhsT=qk_raw[32 * h:32 * h + 32, 0, :],
                       rhs=qk_raw[32 * h:32 * h + 32, 1, :], start=True, stop=True).then_inc(gprod_done, 1)
            def phase1(n, a, do):
                if not do[0] and do[1]: y_weights()
                if do[3]: bias_of(n - 3, 1 - a)
                if do[2]:
                    need(pe, xs_made, n - 3)
                    pe.wait_ge(lo_ready, n - 1)
                    turn(T2, a, turned16[a]).then_inc(t1_done, 1)

            pe.wait_ge(wb_ready, 1)
            run_phase1(pe, phase1)

            pe.wait_ge(w_ready, 1)
            pe.wait_ge(b_evac, PAIRS - 1)

            def y_of(g, c, h, a, bank=ps_y):
                i = 8 * g + 4 * c + h
                if c == 0 and h == 0:
                    pe.wait_ge(xs_loaded[a], 16 * g + 32 - 16 * a)
                if bank is ps_y:
                    need(pe, ylo_done, i)
                cols = xs[a][:, CH * c:CH * c + CH]
                mm(bank[:, 0:CH], lhsT=g_hi[:, h, :], rhs=cols, start=True, stop=False)
                mm(bank[:, 0:CH], lhsT=g_lo[:, h, :], rhs=cols, start=False, stop=True).then_inc(y_done, 1)

            def scores(n, r, u, a):
                q, c, off = 4 * n + r, r // 2, (r % 2) * N
                pe.wait_ge(ylo_done, 8 * n + 4 * c + 4)
                need(pe, exp_done, 2 * q + u + 1 - 4)
                full, part = xs[a][:, N * r:N * r + N], xs_mask[a][:, N * r:N * r + N]
                for k in ((0, 1, 2), (3,))[u]:
                    o = ps_scores[r % 2][u][:, (k % 3) * N:(k % 3) * N + N]
                    mm(o, lhsT=y_hi[c][:, k, off:off + P], rhs=full, start=True, stop=False)
                    mm(o, lhsT=y_lo[c][:, k, off:off + P], rhs=part, start=False, stop=False)
                    mm(o, lhsT=ident16[:], rhs=bias_hi[:, k, :], start=False, stop=False)
                    last = mm(o, lhsT=ident16[:], rhs=bias_lo[:, k, :], start=False, stop=True)
                if u == 1:
                    for h in range(H):
                        o = ps_scores[r % 2][1][32 * h:32 * h + 32, N:2 * N]
                        mm(o, lhsT=y_hi[c][:, h, off + P:off + N], rhs=full, start=True, stop=False)
                        mm(o, lhsT=y_lo[c][:, h, off + P:off + N], rhs=part, start=False, stop=False)
                    o = ps_scores[r % 2][1][:, N:2 * N]
                    mm(o, lhsT=ident16[:], rhs=bias_hi[:, H, :], start=False, stop=False)
                    last = mm(o, lhsT=ident16[:], rhs=bias_lo[:, H, :], start=False, stop=True)
                last.then_inc(s_done, 1)

            def alpha(n, r):
                q, a = 4 * n + r, r % 2
                pe.wait_ge(pnm_done, q + 1)
                need(pe, ptm_done, q)
                for h in range(H):
                    last = pe.transpose(ps_pt[:, P * h:P * h + P], pn_main[a][:, h, :], ident[:])
                last.then_inc(alpha_done, 1)

            def beta(n, r):
                q, a = 4 * n + r, r % 2
                pe.wait_ge(pnp_done, q + 1)
                pe.wait_ge(pnr_done, q + 1)
                need(pe, ptb_done, 2 * q)
                need(pe, og_done, q - 1)
                pe.transpose(ps_o[:, N:N + P], pn_pack[a][:, 0:P], ident[:])
                pe.transpose(ps_o[:, N + P:N + 2 * P], pn_rest[a][:].rearrange("i h j -> i (h j)"), ident[:]).then_inc(beta_done, 1)

            def attend(n, r, a, more_beta):
                q, b = 4 * n + r, r % 2
                pe.wait_ge(ptm_done, q + 1)
                pe.wait_ge(tr_done, q + 1)
                if more_beta:
                    pe.wait_ge(ptb_done, 2 * q + 4)
                else:
                    pe.wait_ge(ptb_done, 2 * q + 2)
                pe.wait_ge(v_evac, n + 1)
                pe.wait_ge(vr_evac, n + 1)
                need(pe, og_done, q)
                for h in range(H):
                    mm(ps_o[32 * h:32 * h + 32, 0:N], lhsT=v_main[a][:, r, 32 * h:32 * h + 32], rhs=pt_main[b][:, h, :],
                       start=True, stop=False)
                mm(ps_o[:, 0:N], lhsT=v_bd[a][:, r].rearrange("j h e -> j (h e)"), rhs=pt_pack[b][:], start=False, stop=True).then_inc(av_done, 1)

            reader = [None, 0]

            def take_m(sem_, value):
                if reader[0] is not None:
                    need(pe, *reader)
                reader[:] = sem_, value

            def project_v(n, a):
                take_m(v_evac, n + 1)
                for r in range(RG):
                    cols = xs[a][:, N * r:N * r + P]
                    mm(ps_m[:, P * r:P * r + P], lhsT=cols, rhs=w_hi[:, V0:V0 + P], start=True, stop=False)
                    last = mm(ps_m[:, P * r:P * r + P], lhsT=cols, rhs=w_lo[:, V0:V0 + P], start=False, stop=True)
                last.then_inc(v_done, 1)

            def project_v_rest(n, a):
                take_m(vr_evac, n + 1)
                for r in range(RG):
                    cols = xs[a][:, N * r + P:N * r + N]
                    for h in range(H):
                        o = ps_m[32 * h:32 * h + 32, DH * r:DH * r + DH]
                        mm(o, lhsT=cols, rhs=w_hi[:, V0 + DH * h:V0 + DH * h + DH], start=True, stop=False)
                        last = mm(o, lhsT=cols, rhs=w_lo[:, V0 + DH * h:V0 + DH * h + DH], start=False, stop=True)
                last.then_inc(vr_done, 1)

            def project_gate(n, a, c):
                take_m(g_evac, 2 * n + c + 1)
                cols = xs[a][:, CH * c:CH * c + CH]
                mm(ps_m[:, 0:CH], lhsT=w_hi[:, G0:G0 + P], rhs=cols, start=True, stop=False)
                mm(ps_m[:, 0:CH], lhsT=w_lo[:, G0:G0 + P], rhs=cols, start=False, stop=True).then_inc(g_done, 1)

            def turn2(g, a):
                take_m(xs2_done, g + 1)
                pe.wait_ge(lo2_ready, g + 1)
                turn(T, a, [ps_m16]).then_inc(t2_done, 1)

            def router(g):
                take_m(lg_done, g + 1)
                pe.wait_ge(xs2_done, g + 1)
                for t in range(T):
                    mm(ps_m[:, E * t:E * t + E], lhsT=xs2[:, t, :], rhs=w_hi[:, R0:R0 + E], start=True, stop=False)
                    last = mm(ps_m[:, E * t:E * t + E], lhsT=xs2[:, t, :], rhs=w_lo[:, R0:R0 + E], start=False, stop=True)
                last.then_inc(rt_done, 1)

            def project_out(g):
                take_m(x1_done, g + 1)
                pe.wait_ge(ogl_done, 4 * g + 4)
                for t in range(T):
                    o = ps_m[:, D * t:D * t + D]
                    mm(o, lhsT=og_hi[:, t:TG:T], rhs=w_hi[:, O0:O0 + D], start=True, stop=False)
                    mm(o, lhsT=og_hi[:, t:TG:T], rhs=w_lo[:, O0:O0 + D], start=False, stop=False)
                    last = mm(o, lhsT=og_lo[:, t:TG:T], rhs=w_hi[:, O0:O0 + D], start=False, stop=True)
                last.then_inc(wo_done, 1)

            def experts(g, t, busy):
                bank = expert_bank(t, busy)
                if bank is ps_m:
                    take_m(prod_done, 5 * g + t + 1)
                else:
                    pe.wait_ge(exp_done, 8 * GROUPS - 2)
                    need(pe, prod_done, 5 * g + t - 1)
                mm(bank[:], lhsT=xs2[:, t, :], rhs=w_hi[:, X0:X0 + 512], start=True, stop=False)
                mm(bank[:], lhsT=xs2[:, t, :], rhs=w_lo[:, X0:X0 + 512], start=False, stop=True).then_inc(e_done, 1)

            def turn_coef(g):
                take_m(ct_evac, g + 1)
                pe.wait_ge(rt_step, 19 * g + 19)
                pe.transpose(ps_m16[:, 0:P], c_stack[:], ident16[:]).then_inc(ct_done, 1)

            def expert_bias(g):
                take_m(res_done, g + 1)
                pe.wait_ge(ct_evac, g + 1)
                for t in range(T):
                    last = mm(ps_m[:, D * t:D * t + D], lhsT=c_t[:], rhs=eb_sel[:, t, :], start=True, stop=True)
                last.then_inc(cb_done, 1)

            def step(n, a, do):
                att, wo, ex, fin, more = do
                b = 1 - a
                if isinstance(n, int) and n == 1:
                    reader[:] = g_evac, 2 * n
                elif isinstance(n, int) and n == GROUPS + 2:
                    reader[:] = res_done, n - 3
                elif not isinstance(n, int) or n > 1:
                    reader[:] = x1_done, n - 1
                if att: scores(n, 0, 0, a)
                if att: project_v(n, a)
                if att: y_of(n, 1, 0, a)
                if wo: beta(n - 1, 2)
                if att: scores(n, 0, 1, a)
                if att: project_v_rest(n, a)
                if wo: alpha(n - 1, 2)
                if att: y_of(n, 1, 1, a)
                if att: project_gate(n, a, 0)
                if wo: attend(n - 1, 1, b, wo)
                if att: y_of(n, 1, 2, a)
                if att: project_gate(n, a, 1)
                if att: scores(n, 1, 0, a)
                if fin: experts(n - 3, 0, att)
                if att: y_of(n, 1, 3, a)
                if att: scores(n, 1, 1, a)
                if fin: experts(n - 3, 1, att)
                if wo: beta(n - 1, 3)
                if wo: alpha(n - 1, 3)
                if fin: experts(n - 3, 2, att)
                if more: y_of(n + 1, 0, 0, b)
                if wo: attend(n - 1, 2, b, wo)
                if fin: experts(n - 3, 3, att)
                if att: scores(n, 2, 0, a)
                if fin: experts(n - 3, 4, att)
                if more: y_of(n + 1, 0, 1, b)
                if att: scores(n, 2, 1, a)
                if ex: turn2(n - 2, a)
                if att: alpha(n, 0)
                if more: y_of(n + 1, 0, 2, b)
                if att: beta(n, 0)
                if fin: turn_coef(n - 3)
                if att: scores(n, 3, 0, a)
                if wo: attend(n - 1, 3, b, att)
                if ex: router(n - 2)
                if more: y_of(n + 1, 0, 3, b)
                if att: beta(n, 1)
                if fin: expert_bias(n - 3)
                if att: scores(n, 3, 1, a)
                if att: alpha(n, 1)
                if att: attend(n, 0, a, att)
                if wo: project_out(n - 1)

            for h in range(H):
                y_of(0, 0, h, 0, first_y[h])
            pe.wait_ge(b_ready, 1)
            run_steps(pe, step)


_INS = ["x", "WqT", "WkT", "Wv", "Wg", "Wo", "Wb", "router_w", "router_b", "expert_w", "expert_b", "mask"]


def kernel(x, L0_conv_mask, L0_conv_Wq, L0_conv_Wk, L0_conv_Wv, L0_conv_Wg, L0_conv_Wo, L0_conv_Wb,
           L0_ffn_router_w, L0_ffn_router_b, L0_ffn_expert_w, L0_ffn_expert_b):
    import numpy as np
    import concourse.bacc as bacc
    from concourse.bass_utils import run_bass_kernel_spmd

    turned = lambda w: np.concatenate([np.asarray(w).T, np.asarray(w).T], axis=1)
    given = {"x": x, "WqT": turned(L0_conv_Wq), "WkT": turned(L0_conv_Wk), "Wv": L0_conv_Wv, "Wg": L0_conv_Wg,
             "Wo": L0_conv_Wo, "Wb": L0_conv_Wb, "router_w": L0_ffn_router_w, "router_b": L0_ffn_router_b,
             "expert_w": L0_ffn_expert_w, "expert_b": L0_ffn_expert_b, "mask": np.asarray(L0_conv_mask).view(np.uint8)}
    nc = bacc.Bacc("TRN2", target_bir_lowering=False, num_devices=1)
    arrays, args = {}, []
    for name in _INS:
        a = np.ascontiguousarray(given[name])
        arrays[f"in_{name}"] = a
        args.append(nc.dram_tensor(f"in_{name}", a.shape, mybir.dt.from_np(a.dtype), kind="ExternalInput").ap())
    out = nc.dram_tensor("out_0", np.asarray(x).shape, F32, kind="ExternalOutput").ap()
    build(nc, *args, out)
    r = run_bass_kernel_spmd(nc, [arrays], core_ids=[0])
    return r.results[0]["out_0"]
```
